# Optimizing a Trainium2 kernel written in Bass

```python
import numpy as np
import jax
import jax.numpy as jnp

def _softmax(x, axis=-1):
    return jax.nn.softmax(x, axis=axis)

def _gelu(x):
    return jax.nn.gelu(x, approximate=True)

def _silu(x):
    return jax.nn.silu(x)

def _sigmoid(x):
    return jax.nn.sigmoid(x)

def _layernorm(x, axis=-1, eps=1e-05):
    m = jnp.mean(x, axis=axis, keepdims=True)
    v = jnp.var(x, axis=axis, keepdims=True)
    return (x - m) / jnp.sqrt(v + eps)

def _scatter_add(tgt, idx, src, axis=0):
    return tgt.at[idx].add(src)

def _segment_sum(src, seg, n):
    return jax.ops.segment_sum(src, seg, n)
kernel_name = 'mk_flamingo_gated_d2_seqx_r8_d456e7'

def setup_inputs(seed: int=0):
    np.random.seed(seed)
    _w = jnp.asarray

    def _rec_inputs():
        import jax
        import jax.numpy as jnp
        _rk = jax.random.key(seed)
        x = 7.22e-05 + 1 * jax.random.normal(jax.random.fold_in(_rk, 1), (16, 64, 512), jnp.float32)
        _lenS = 64 - jax.random.randint(jax.random.fold_in(_rk, 7), (16,), 0, max(1, 64 // 4) + 1, jnp.int32)
        _lenS2 = 64 - jax.random.randint(jax.random.fold_in(_rk, 8), (16,), 0, max(1, 64 // 4) + 1, jnp.int32)
        _ctx_4096P = jax.random.normal(jax.random.fold_in(_rk, 11), (16, 16, 512), jnp.float32)
        _ctx_4096c = jax.random.dirichlet(jax.random.fold_in(_rk, 511), 0.3 * jnp.ones((16,), jnp.float32), (16, 64))
        _ctx_4096t = jnp.einsum('bsk,bkd->bsd', _ctx_4096c, _ctx_4096P)
        _ctx_4096t = _ctx_4096t * jax.lax.rsqrt(jnp.mean(jnp.square(_ctx_4096t)) + 1e-12) * 0.953939
        ctx_4096 = 4.13588e-05 + 0.999923 * (_ctx_4096t + 0.3 * jax.random.normal(jax.random.fold_in(_rk, 611), (16, 64, 512), jnp.float32))
        _g = jax.random.normal(jax.random.fold_in(_rk, 9001), (2, 2), jnp.float32)
        _g = jnp.sign(_g) * jnp.maximum(jnp.abs(_g), 1.0) + (_g == 0) * 1.0
        g_xattn = _g[0]
        g_ffn = _g[1]
        return (x, ctx_4096, g_xattn, g_ffn)
    x, ctx_4096, g_xattn, g_ffn = _rec_inputs()

    def _L0_xattn_setup():
        import jax, jax.numpy as jnp
        import numpy as np
        B, C, T = (4, 64, 512)
        DQK = 64
        key = jax.random.key(seed)
        ks = jax.random.split(key, 8)
        s = 1.0 / np.sqrt(C)
        return {'x': jax.random.normal(ks[0], (B, C, T), dtype=jnp.float32), 'init': jax.random.normal(ks[1], (B, C, T), dtype=jnp.float32), 'Wq': jax.random.normal(ks[2], (DQK, C), dtype=jnp.float32) * s, 'bq': jax.random.normal(ks[3], (DQK,), dtype=jnp.float32) * s, 'Wk': jax.random.normal(ks[4], (DQK, C), dtype=jnp.float32) * s, 'bk': jax.random.normal(ks[5], (DQK,), dtype=jnp.float32) * s, 'Wv': jax.random.normal(ks[6], (C, C), dtype=jnp.float32) * s, 'bv': jax.random.normal(ks[7], (C,), dtype=jnp.float32) * s}
    _L0_xattn_all = _L0_xattn_setup()
    _L0_xattn_in = {k: v for k, v in _L0_xattn_all.items() if k in ('Wq', 'bq', 'Wk', 'bk', 'Wv', 'bv')}
    del _L0_xattn_all

    def _L0_ffn_setup():
        import jax, jax.numpy as jnp
        import numpy as np
        B, T, D_IN, D_OUT = (8, 256, 512, 512)
        N_LORAS, RANK = (16, 32)
        SCALING = 1.0
        key = jax.random.key(seed)
        ks = jax.random.split(key, 8)
        std = 1.0 / D_IN ** 0.5
        x = jax.random.normal(ks[0], (B, T, D_IN), dtype=jnp.float32)
        idx = jax.random.randint(ks[1], (B,), 0, N_LORAS)
        gate = jax.nn.one_hot(idx, N_LORAS, dtype=jnp.float32)
        kernel = jax.random.normal(ks[2], (D_IN, D_OUT), dtype=jnp.float32) * std
        bias = jnp.zeros((D_OUT,), dtype=jnp.float32)
        lora_A = jax.random.normal(ks[3], (N_LORAS, RANK, D_IN), dtype=jnp.float32) * std
        lora_B = jax.random.normal(ks[4], (N_LORAS, D_OUT, RANK), dtype=jnp.float32) * 0.01
        lora_A_shared = jax.random.normal(ks[5], (RANK, D_IN), dtype=jnp.float32) * std
        lora_B_shared = jax.random.normal(ks[6], (D_OUT, RANK), dtype=jnp.float32) * 0.01
        return {'x': x, 'gate': gate, 'kernel': kernel, 'bias': bias, 'lora_A': lora_A, 'lora_B': lora_B, 'lora_A_shared': lora_A_shared, 'lora_B_shared': lora_B_shared}
    _L0_ffn_all = _L0_ffn_setup()
    _L0_ffn_in = {k: v for k, v in _L0_ffn_all.items() if k in ('gate', 'kernel', 'bias', 'lora_A', 'lora_B', 'lora_A_shared', 'lora_B_shared')}
    del _L0_ffn_all

    def _L1_xattn_setup():
        import jax, jax.numpy as jnp
        import numpy as np
        NUM_HEADS = 8

        def _proj(W, b, x):
            return jnp.einsum('oi,bil->bol', W, x) + b[:, None]
        key = jax.random.key(seed)
        ks = jax.random.split(key, 11)
        B, D, L = (16, 64, 512)
        s = 1.0 / np.sqrt(D).astype(np.float32)
        return {'x_query': jax.random.normal(ks[0], (B, D, L), jnp.float32), 'x_key': jax.random.normal(ks[1], (B, D, L), jnp.float32), 'x_value': jax.random.normal(ks[2], (B, D, L), jnp.float32), 'Wq': jax.random.normal(ks[3], (D, D), jnp.float32) * s, 'bq': jax.random.normal(ks[4], (D,), jnp.float32) * 0.01, 'Wk': jax.random.normal(ks[5], (D, D), jnp.float32) * s, 'bk': jax.random.normal(ks[6], (D,), jnp.float32) * 0.01, 'Wv': jax.random.normal(ks[7], (D, D), jnp.float32) * s, 'bv': jax.random.normal(ks[8], (D,), jnp.float32) * 0.01, 'Wo': jax.random.normal(ks[9], (D, D), jnp.float32) * s, 'bo': jax.random.normal(ks[10], (D,), jnp.float32) * 0.01}
    _L1_xattn_all = _L1_xattn_setup()
    _L1_xattn_in = {k: v for k, v in _L1_xattn_all.items() if k in ('Wq', 'bq', 'Wk', 'bk', 'Wv', 'bv', 'Wo', 'bo')}
    del _L1_xattn_all

    def _L1_ffn_setup():
        import jax, jax.numpy as jnp
        import numpy as np
        BLOCK_SIZE = 64
        OUT_F, IN_F = (512, 512)

        def dequantize(qweights, scales, block_size=BLOCK_SIZE):
            shape = qweights.shape
            n = qweights.size
            flat = qweights.reshape(-1)
            pad = -n % block_size
            if pad:
                flat = jnp.pad(flat, (0, pad))
            blocks = flat.reshape(-1, block_size).astype(scales.dtype) * scales
            return blocks.reshape(-1)[:n].reshape(shape)
        key = jax.random.key(seed)
        k_x, k_w, k_s, k_b = jax.random.split(key, 4)
        x = jax.random.normal(k_x, (4, 256, 512), dtype=jnp.float32)
        quantized_weights = jax.random.randint(k_w, (OUT_F, IN_F), -128, 128, dtype=jnp.int32).astype(jnp.int8)
        n_blocks = (OUT_F * IN_F + BLOCK_SIZE - 1) // BLOCK_SIZE
        scale_values = jax.random.uniform(k_s, (n_blocks, 1), minval=0.001, maxval=0.02, dtype=jnp.float32)
        bias = jax.random.normal(k_b, (OUT_F,), dtype=jnp.float32) * 0.02
        return {'x': x, 'quantized_weights': quantized_weights, 'scale_values': scale_values, 'bias': bias}
    _L1_ffn_all = _L1_ffn_setup()
    _L1_ffn_in = {k: v for k, v in _L1_ffn_all.items() if k in ('quantized_weights', 'scale_values', 'bias')}
    del _L1_ffn_all
    return {'x': x, 'ctx_4096': ctx_4096, 'g_xattn': g_xattn, 'g_ffn': g_ffn, 'L0_xattn_Wq': _L0_xattn_in['Wq'], 'L0_xattn_bq': _L0_xattn_in['bq'], 'L0_xattn_Wk': _L0_xattn_in['Wk'], 'L0_xattn_bk': _L0_xattn_in['bk'], 'L0_xattn_Wv': _L0_xattn_in['Wv'], 'L0_xattn_bv': _L0_xattn_in['bv'], 'L0_ffn_gate': _L0_ffn_in['gate'], 'L0_ffn_kernel': _L0_ffn_in['kernel'], 'L0_ffn_bias': _L0_ffn_in['bias'], 'L0_ffn_lora_A': _L0_ffn_in['lora_A'], 'L0_ffn_lora_B': _L0_ffn_in['lora_B'], 'L0_ffn_lora_A_shared': _L0_ffn_in['lora_A_shared'], 'L0_ffn_lora_B_shared': _L0_ffn_in['lora_B_shared'], 'L1_xattn_Wq': _L1_xattn_in['Wq'], 'L1_xattn_bq': _L1_xattn_in['bq'], 'L1_xattn_Wk': _L1_xattn_in['Wk'], 'L1_xattn_bk': _L1_xattn_in['bk'], 'L1_xattn_Wv': _L1_xattn_in['Wv'], 'L1_xattn_bv': _L1_xattn_in['bv'], 'L1_xattn_Wo': _L1_xattn_in['Wo'], 'L1_xattn_bo': _L1_xattn_in['bo'], 'L1_ffn_quantized_weights': _L1_ffn_in['quantized_weights'], 'L1_ffn_scale_values': _L1_ffn_in['scale_values'], 'L1_ffn_bias': _L1_ffn_in['bias']}

def reference(x, ctx_4096, g_xattn, g_ffn, L0_xattn_Wq, L0_xattn_bq, L0_xattn_Wk, L0_xattn_bk, L0_xattn_Wv, L0_xattn_bv, L0_ffn_gate, L0_ffn_kernel, L0_ffn_bias, L0_ffn_lora_A, L0_ffn_lora_B, L0_ffn_lora_A_shared, L0_ffn_lora_B_shared, L1_xattn_Wq, L1_xattn_bq, L1_xattn_Wk, L1_xattn_bk, L1_xattn_Wv, L1_xattn_bv, L1_xattn_Wo, L1_xattn_bo, L1_ffn_quantized_weights, L1_ffn_scale_values, L1_ffn_bias):
    import jax
    import jax.numpy as jnp

    def _L0_xattn_ref(x, init, Wq, bq, Wk, bk, Wv, bv):
        import jax, jax.numpy as jnp
        import numpy as np
        B, C, T = (4, 64, 512)
        DQK = 64
        q = jnp.einsum('dc,bct->btd', Wq, init) + bq
        k = jnp.einsum('dc,bct->bdt', Wk, init) + bk[None, :, None]
        R = jnp.einsum('btd,bds->bts', q, k)
        attention = jax.nn.softmax(R, axis=-1)
        v = jnp.einsum('oc,bct->bto', Wv, x) + bv
        out = jnp.einsum('bts,bsc->bct', attention, v)
        return out

    def _L0_ffn_ref(x, gate, kernel, bias, lora_A, lora_B, lora_A_shared, lora_B_shared):
        import jax, jax.numpy as jnp
        import numpy as np
        B, T, D_IN, D_OUT = (8, 256, 512, 512)
        N_LORAS, RANK = (16, 32)
        SCALING = 1.0
        base_out = jnp.matmul(x, kernel) + bias
        b = gate.shape[0]
        x_flat = x.reshape(b, -1, x.shape[-1])
        A_eff = jnp.einsum('bn,nri->bri', gate, lora_A)
        B_eff = jnp.einsum('bn,nor->bor', gate, lora_B)
        Ax = jnp.einsum('bri,bti->btr', A_eff, x_flat)
        delta_flat = jnp.einsum('bor,btr->bto', B_eff, Ax)
        Ax_s = jnp.einsum('ri,bti->btr', lora_A_shared, x_flat)
        delta_flat = delta_flat + jnp.einsum('or,btr->bto', lora_B_shared, Ax_s)
        delta = delta_flat.reshape(x.shape[:-1] + (kernel.shape[-1],))
        return base_out + (SCALING * delta).astype(base_out.dtype)

    def _L1_xattn_ref(x_query, x_key, x_value, Wq, bq, Wk, bk, Wv, bv, Wo, bo):
        import jax, jax.numpy as jnp
        import numpy as np
        NUM_HEADS = 8

        def _proj(W, b, x):
            return jnp.einsum('oi,bil->bol', W, x) + b[:, None]
        B, D, L = x_query.shape
        h = NUM_HEADS
        Lh = L // h
        q = _proj(Wq, bq, x_query)
        k = _proj(Wk, bk, x_key)
        v = _proj(Wv, bv, x_value)
        qh = q.reshape(B, D, h, Lh).transpose(2, 0, 1, 3)
        kh = k.reshape(B, D, h, Lh).transpose(2, 0, 1, 3)
        vh = v.reshape(B, D, h, Lh).transpose(2, 0, 1, 3)
        scale = 1.0 / jnp.sqrt(jnp.asarray(Lh, x_query.dtype))
        scores = jnp.einsum('hbdk,hbek->hbde', qh, kh) * scale
        p = jax.nn.softmax(scores, axis=-1)
        xh = jnp.einsum('hbde,hbek->hbdk', p, vh)
        x = xh.transpose(1, 2, 0, 3).reshape(B, D, L)
        return _proj(Wo, bo, x)

    def _L1_ffn_ref(x, quantized_weights, scale_values, bias):
        import jax, jax.numpy as jnp
        import numpy as np
        BLOCK_SIZE = 64
        OUT_F, IN_F = (512, 512)

        def dequantize(qweights, scales, block_size=BLOCK_SIZE):
            shape = qweights.shape
            n = qweights.size
            flat = qweights.reshape(-1)
            pad = -n % block_size
            if pad:
                flat = jnp.pad(flat, (0, pad))
            blocks = flat.reshape(-1, block_size).astype(scales.dtype) * scales
            return blocks.reshape(-1)[:n].reshape(shape)
        w_fp = dequantize(quantized_weights, scale_values)
        return jnp.einsum('bsi,oi->bso', x, w_fp) + bias
    x = x + jnp.tanh(g_xattn[0]) * _L0_xattn_ref(_layernorm(x, axis=-1), ctx_4096, L0_xattn_Wq, L0_xattn_bq, L0_xattn_Wk, L0_xattn_bk, L0_xattn_Wv, L0_xattn_bv)
    x = x + jnp.tanh(g_ffn[0]) * _L0_ffn_ref(_layernorm(x, axis=-1), L0_ffn_gate, L0_ffn_kernel, L0_ffn_bias, L0_ffn_lora_A, L0_ffn_lora_B, L0_ffn_lora_A_shared, L0_ffn_lora_B_shared)
    x = x + jnp.tanh(g_xattn[1]) * _L1_xattn_ref(_layernorm(x, axis=-1), ctx_4096, ctx_4096, L1_xattn_Wq, L1_xattn_bq, L1_xattn_Wk, L1_xattn_bk, L1_xattn_Wv, L1_xattn_bv, L1_xattn_Wo, L1_xattn_bo)
    x = x + jnp.tanh(g_ffn[1]) * _L1_ffn_ref(_layernorm(x, axis=-1), L1_ffn_quantized_weights, L1_ffn_scale_values, L1_ffn_bias)
    return x

_drawn_inputs = setup_inputs


def setup_inputs(seed=0):
    import zlib

    import numpy as np

    out = dict(_drawn_inputs(seed))
    spreads = {'g_ffn': (-1.0, 0.2), 'L0_ffn_bias': (0.0, 0.1)}
    factors = {'L0_xattn_bk': 64.0,
     'L0_xattn_bv': 8.0,
     'L1_xattn_bq': 35.235,
     'L1_xattn_bk': 32.774,
     'L1_xattn_bv': 61.497,
     'L1_xattn_bo': 64.0,
     'L1_ffn_bias': 60.253}
    for name, (base, spread) in spreads.items():
        noise = np.random.default_rng([zlib.crc32(name.encode()), seed]).standard_normal(out[name].shape)
        drawn = base * np.exp(spread * noise) if base else spread * noise
        out[name] = jnp.asarray(drawn.astype(out[name].dtype))
    for name, factor in factors.items():
        out[name] = (out[name] * factor).astype(out[name].dtype)
    return out
```

```python
from contextlib import ExitStack

import concourse.bass as bass
from concourse import mybir

F32 = mybir.dt.float32
F32R = mybir.dt.float32r
I8 = mybir.dt.int8
I32 = mybir.dt.int32
ALU = mybir.AluOpType
ACT = mybir.ActivationFunctionType
AX = mybir.AxisListType

P = 128
C = 64
T = 512
NB = 16
PAIRS = NB * C // P
KC = T // P
H = 8
E = T // H
NL, R = 16, 32
QB_ = 64
EPS = 1e-5
Q1 = C + 1


def flamingo_two_layers(nc, a, out):
    with ExitStack() as ctx:
        def sb(name, shape, dt=F32):
            return ctx.enter_context(nc.sbuf_tensor(name, shape, dt))

        def ps(name, shape):
            return ctx.enter_context(nc.psum_tensor(name, shape, F32))

        def sem(name):
            return ctx.enter_context(nc.semaphore(name))

        scores = [ps("scores0", [P, 2, T]), ps("scores1", [P, 2, T])]
        bank_a = ps("bank_a", [P, T])
        bank_b = ps("bank_b", [P, T])
        gen = ps("gen", [P, 2, T])
        g6, g7 = gen[:, 0, :], gen[:, 1, :]

        ident = sb("ident", [P, P])
        ones = sb("ones", [P, C])
        neg_half = sb("neg_half", [P, 1])
        gates = sb("gates", [P, 4])
        tg = sb("tg", [P, 4])
        GX0, GX1, GF0, GF1 = range(4)
        wq_twice = sb("wq_twice", [C, 2, C])
        wk_bk = sb("wk_bk", [C, Q1])
        bq0 = sb("bq0", [C, 1])
        m_hi = sb("m_hi", [P, Q1], F32R)
        m_lo = sb("m_lo", [C, Q1], F32R)
        qk_bias = sb("qk_bias", [Q1, 1])
        diag = sb("diag", [P, 5, P])
        diag_t = sb("diag_t", [P, 5, P])
        V0, WQ, WK, WV, WO = range(5)
        bv0_row = sb("bv0_row", [P, 2, C])
        bq1_row = sb("bq1_row", [P, 2, C])
        bk1_row = sb("bk1_row", [P, 2, C])
        bv1_col = sb("bv1_col", [P, 1])
        bo_col = sb("bo_col", [P, 1])
        kern = sb("kern", [P, KC, T])
        kern_hi = sb("kern_hi", [P, KC, T], F32R)
        kern_lo = sb("kern_lo", [P, KC, T], F32R)
        lora_a = sb("lora_a", [P, KC, T])
        lora_b = sb("lora_b", [P, C, R])
        share_a = sb("share_a", [R, T])
        share_b = sb("share_b", [P, KC, R])
        gate_t = sb("gate_t", [NL, PAIRS])
        sel_a = sb("sel_a", [NL, KC, 4, R])
        sel_b = sb("sel_b", [NL, NL, PAIRS])
        gate_p = sb("gate_p", [P, 5 * PAIRS])
        eq_r = sb("eq_r", [P, R])
        eq_o = sb("eq_o", [P, PAIRS])
        mix_a = sb("mix_a", [P, KC * PAIRS, R])
        mix_b = sb("mix_b", [P, PAIRS, PAIRS])
        ae_hi = sb("ae_hi", [P, PAIRS, KC, R], F32R)
        ae_lo = sb("ae_lo", [P, PAIRS, KC, R], F32R)
        low_a_hi = sb("low_a_hi", [P, KC, Q1 + 1], F32R)
        low_a_lo = sb("low_a_lo", [P, KC, Q1 + 1], F32R)
        low_b = sb("low_b", [Q1, PAIRS, T])
        share_bt = sb("share_bt", [2 * R, T])
        q_words = sb("q_words", [P, KC, T // 4], I32)
        q8 = q_words[:].rearrange("p k w -> p (k w)").bitcast(I8).rearrange("p (k i) -> p k i", k=KC)
        q_scale = sb("q_scale", [P, KC, T // QB_])
        w1_hi = sb("w1_hi", [P, KC, T], F32R)
        w1_lo = sb("w1_lo", [P, KC, T], F32R)
        b1_row = sb("b1_row", [P, T])

        x_ln = sb("x_ln", [P, T])
        x_res = sb("x_res", [P, T])
        ctx2 = sb("ctx2", [P, 2, T])
        ca = sb("ca", [Q1, 2, T], F32R)
        cb = sb("cb", [P, 2, T], F32R)
        qa = sb("qa", [Q1, 2, T], F32R)
        qb = sb("qb", [P, 2, T], F32R)
        neg_max = sb("neg_max", [P, 2, KC])
        prob = sb("prob", [P, 2, KC, T])
        half = sb("half", [P, 2, 2, T])
        prob_sum = sb("prob_sum", [P, 2, T])
        v0 = sb("v0", [P, KC, P])
        recip = sb("recip", [P, T])
        att = sb("att", [P, T])
        x1 = sb("x1", [P, T])
        stats = [sb(f"stats{i}", [P, 6]) for i in range(4)]
        mean_var = [sb(f"mean_var{i}", [P, 2]) for i in range(4)]
        var_eps = [sb(f"var_eps{i}", [P, 1]) for i in range(4)]
        rstd = [sb(f"rstd{i}", [P, 1]) for i in range(4)]
        norm = [sb(f"norm{i}", [P, T]) for i in range(4)]
        ctx1 = sb("ctx1", [P, T])
        xt_hi = sb("xt_hi", [P, KC, P], F32R)
        xt_lo = sb("xt_lo", [P, KC, P], F32R)
        low = sb("low", [Q1, P])
        x2 = sb("x2", [P, T])
        k1t = sb("k1t", [P, KC, P])
        q1t = sb("q1t", [P, KC, P])
        v1 = sb("v1", [P, T])
        head_max = sb("head_max", [P, H])
        shifted = sb("shifted", [P, H, E])
        prob1 = sb("prob1", [P, H, E])
        head_sum = sb("head_sum", [P, H])
        head_rec = sb("head_rec", [P, H])
        prob1t = sb("prob1t", [P, H, E])
        heads = sb("heads", [P, T])
        x3 = sb("x3", [P, T])
        x3b = sb("x3b", [P, T])
        yt_hi = sb("yt_hi", [P, KC, P], F32R)
        yt_lo = sb("yt_lo", [P, KC, P], F32R)
        x4 = sb("x4", [P, T])

        w_small = sem("w_small")
        w_ffn0 = sem("w_ffn0")
        w_lora = sem("w_lora")
        w_ffn1 = sem("w_ffn1")
        pool_const = sem("pool_const")
        dve_const = sem("dve_const")
        pool_zero = sem("pool_zero")
        tg_done = sem("tg_done")
        m_ready = sem("m_ready")
        m_done = sem("m_done")
        m_hi_done = sem("m_hi_done")
        diag_ready = sem("diag_ready")
        diag_done = sem("diag_done")
        row_bias_done = sem("row_bias_done")
        kern_hi_done = sem("kern_hi_done")
        kern_lo_done = sem("kern_lo_done")
        gate_ready = sem("gate_ready")
        gate_done = sem("gate_done")
        mix_done = sem("mix_done")
        ae_ready = sem("ae_ready")
        ae_hi_done = sem("ae_hi_done")
        ae_lo_done = sem("ae_lo_done")
        be_ready = sem("be_ready")
        be_done = sem("be_done")
        sh_ready = sem("sh_ready")
        sh_done = sem("sh_done")
        low_b_done = sem("low_b_done")
        w1_deq = sem("w1_deq")
        w1_ready = sem("w1_ready")
        w1_hi_done = sem("w1_hi_done")
        w1_lo_done = sem("w1_lo_done")
        b1_done = sem("b1_done")
        waits_passed = sem("waits_passed")
        x_ln_in = sem("x_ln_in")
        x_res_in = sem("x_res_in")
        ctx2_in = sem("ctx2_in")
        ctx1_in = sem("ctx1_in")
        stored = sem("stored")
        bn_done = [sem(f"bn_done{i}") for i in range(4)]
        mv_done = [sem(f"mv_done{i}") for i in range(4)]
        eps_done = [sem(f"eps_done{i}") for i in range(4)]
        rstd_done = [sem(f"rstd_done{i}") for i in range(4)]
        ln_done = [sem(f"ln_done{i}") for i in range(4)]
        ca_done = sem("ca_done")
        cb_hi_done = sem("cb_hi_done")
        cb_lo_done = sem("cb_lo_done")
        qk_ready = sem("qk_ready")
        qa_done = sem("qa_done")
        qb_done = sem("qb_done")
        nat_ready = sem("nat_ready")
        max_done = sem("max_done")
        row_ready = sem("row_ready")
        row_done = sem("row_done")
        tr_ready = sem("tr_ready")
        exp_done = sem("exp_done")
        half_done = sem("half_done")
        sum_done = sem("sum_done")
        v0_ready = sem("v0_ready")
        v0_done = sem("v0_done")
        num_ready = sem("num_ready")
        den_ready = sem("den_ready")
        recip_done = sem("recip_done")
        att_done = sem("att_done")
        x1_done = sem("x1_done")
        k1_ready = sem("k1_ready")
        k1_done = sem("k1_done")
        v1_ready = sem("v1_ready")
        v1_done = sem("v1_done")
        xt_ready = sem("xt_ready")
        xt_hi_done = sem("xt_hi_done")
        xt_lo_done = sem("xt_lo_done")
        low_a_done = sem("low_a_done")
        low_ready = sem("low_ready")
        low_done = sem("low_done")
        f0_ready = sem("f0_ready")
        x2_done = sem("x2_done")
        q1_ready = sem("q1_ready")
        q1_done = sem("q1_done")
        s1_ready = sem("s1_ready")
        hmax_done = sem("hmax_done")
        shift_done = sem("shift_done")
        p1_done = sem("p1_done")
        hsum_done = sem("hsum_done")
        hrec_done = sem("hrec_done")
        pt_ready = sem("pt_ready")
        pt_done = sem("pt_done")
        o1_ready = sem("o1_ready")
        heads_done = sem("heads_done")
        wo_ready = sem("wo_ready")
        x3_done = sem("x3_done")
        x3b_done = sem("x3b_done")
        yt_ready = sem("yt_ready")
        yt_hi_done = sem("yt_hi_done")
        yt_lo_done = sem("yt_lo_done")
        f1_ready = sem("f1_ready")
        x4_done = sem("x4_done")

        N_SMALL, N_LORA, N_FFN1 = 20, 6, 3

        x_rows = a["x"].rearrange("b c t -> (b c) t")
        c_rows = a["ctx_4096"].rearrange("b c t -> (b c) t")
        o_rows = out.rearrange("b c t -> (b c) t")

        def rows_of(dram, p):
            return dram[bass.ds(p * P, P), :]

        def whole(ap):
            return ap.rearrange("p a b -> p (a b)")

        block = ctx.enter_context(nc.Block())

        def passed(eng):
            eng.sem_inc(waits_passed, 1)

        def run(eng, before, step):
            before()
            step(0, True, False, False)
            step(1, True, True, False)
            with eng.Fori(2, PAIRS) as t:
                step(t, True, True, True)
            step(PAIRS, False, True, True)
            step(PAIRS + 1, False, False, True)

        @block.sync
        def _(sp):
            def load_pair(p, first=False):
                if not first:
                    sp.wait_ge(cb_lo_done, p)
                    sp.wait_ge(ca_done, p)
                for k in range(2):
                    sp.dma_start(ctx2[C * k:C * k + C],
                                 rows_of(c_rows, p).rearrange("(b c) t -> c b t", b=2)).then_inc(ctx2_in, 16)
                if not first:
                    sp.wait_ge(ln_done[0], p)
                sp.dma_start(x_ln[:], rows_of(x_rows, p)).then_inc(x_ln_in, 16)

            def before():
                sp.sem_inc(stored, 16)
                load_pair(0, first=True)
                sp.dma_start(x_res[:], rows_of(x_rows, 0)).then_inc(x_res_in, 16)
                for c in range(KC):
                    sp.dma_start(kern[:, c, :], a["L0_ffn_kernel"][c * P:c * P + P, :]).then_inc(w_ffn0, 16)
                sp.dma_start(lora_a[:], a["L0_ffn_lora_A"].rearrange("(c n) r i -> (n r) c i", n=4)).then_inc(w_lora, 16)
                sp.dma_start(lora_b[:], a["L0_ffn_lora_B"].rearrange("n (a o) r -> (n a) o r", a=PAIRS)).then_inc(w_lora, 16)
                sp.dma_start(share_a[:], a["L0_ffn_lora_A_shared"]).then_inc(w_lora, 16)
                sp.dma_start(share_b[:], a["L0_ffn_lora_B_shared"].rearrange("(k p) r -> p k r", p=P)).then_inc(w_lora, 16)
                sp.dma_start(gate_t[:], a["L0_ffn_gate"].rearrange("b n -> n b"), allow_slow_non_contiguous=True).then_inc(w_lora, 16)
                sp.dma_start(low_b[C:Q1], a["L0_ffn_bias"].unsqueeze(0).unsqueeze(0).broadcast_to([1, PAIRS, T])).then_inc(w_lora, 16)
                sp.dma_start(q_words[:], a["L1_ffn_quantized_weights"].rearrange("(k p) i -> p k i", p=P)).then_inc(w_ffn1, 16)
                sp.dma_start(q_scale[:], a["L1_ffn_scale_values"].rearrange("(k p j) u -> p k (j u)", p=P, k=KC)).then_inc(w_ffn1, 16)
                sp.dma_start(b1_row[:], a["L1_ffn_bias"].partition_broadcast(P)).then_inc(w_ffn1, 16)

            def step(t, A, B, Cc):
                if Cc:
                    sp.wait_ge(x4_done, t - 1)
                    sp.dma_start(rows_of(o_rows, t - 2), x4[:]).then_inc(stored, 16)

            def loads(t, A, B, last=False):
                if A:
                    if not (isinstance(t, int) and t == 0):
                        sp.wait_ge(v1_ready, t)
                    sp.dma_start(ctx1[:], rows_of(c_rows, t)).then_inc(ctx1_in, 16)
                if A and not last:
                    load_pair(t + 1)
                    sp.wait_ge(x1_done, t + 1)
                    sp.dma_start(x_res[:], rows_of(x_rows, t + 1)).then_inc(x_res_in, 16)

            before()
            loads(0, True, False)
            loads(1, True, True)
            with sp.Fori(2, PAIRS - 1) as t:
                loads(t, True, True)
                step(t, True, True, True)
            loads(PAIRS - 1, True, True, last=True)
            step(PAIRS - 1, True, True, True)
            step(PAIRS, False, True, True)
            step(PAIRS + 1, False, False, True)
            sp.wait_ge(stored, 16 * (PAIRS + 1))

        @block.scalar
        def _(act):
            def before():
                def load(dst, src):
                    act.dma_start(dst, src).then_inc(w_small, 16)

                for k in range(2):
                    load(wq_twice[:, k, :], a["L0_xattn_Wq"])
                load(wk_bk[:, 0:C], a["L0_xattn_Wk"])
                load(wk_bk[:, C:Q1], a["L0_xattn_bk"].unsqueeze(1))
                load(bq0[:], a["L0_xattn_bq"].unsqueeze(1))
                load(gates[:, 0:2], a["g_xattn"].partition_broadcast(P))
                load(gates[:, 2:4], a["g_ffn"].partition_broadcast(P))
                for n, name in ((V0, "L0_xattn_Wv"), (WQ, "L1_xattn_Wq"), (WK, "L1_xattn_Wk"),
                                (WV, "L1_xattn_Wv"), (WO, "L1_xattn_Wo")):
                    load(diag[0:C, n, 0:C], a[name])
                    load(diag[C:P, n, C:P], a[name])
                for dst, name in ((bv0_row, "L0_xattn_bv"), (bq1_row, "L1_xattn_bq"), (bk1_row, "L1_xattn_bk")):
                    load(dst[:], a[name].unsqueeze(0).unsqueeze(0).broadcast_to([P, 2, C]))
                act.wait_ge(w_small, 16 * N_SMALL)
                nc.scalar.activation(tg[:], gates[:], ACT.Tanh).then_inc(tg_done, 1)
                for dst, name in ((bv1_col, "L1_xattn_bv"), (bo_col, "L1_xattn_bo")):
                    for k in range(2):
                        act.dma_start(dst[C * k:C * k + C, :], a[name].unsqueeze(1)).then_inc(w_small, 16)

            def prepare_ffn0():
                act.wait_ge(w_ffn0, 16 * KC)
                nc.scalar.activation(kern_hi[:], kern[:], ACT.Copy).then_inc(kern_hi_done, 1)
                for k in range(KC):
                    act.wait_ge(ae_ready, k + 1)
                    nc.scalar.activation(ae_hi[:, :, k, :], gen[:, k % 2, 0:PAIRS * R].rearrange("p (b r) -> p b r", b=PAIRS),
                                         ACT.Copy).then_inc(ae_hi_done, 1)
                act.wait_ge(sh_ready, 1)
                nc.scalar.activation(low_a_hi[:, :, R:2 * R], g6[:, 0:P].rearrange("p (k r) -> p k r", k=KC),
                                     ACT.Copy).then_inc(ae_hi_done, 1)

            def prepare_ffn1():
                for k in range(KC):
                    act.wait_ge(w1_ready, k + 1)
                    nc.scalar.activation(w1_hi[:, k, :], gen[:, k % 2, :], ACT.Copy).then_inc(w1_hi_done, 1)

            def exponentials(t, b, g):
                act.wait_ge(tr_ready, t * 4 + (2 * b + g + 1))
                nc.scalar.activation(prob[:, b, 2 * g:2 * g + 2, :], scores[g][:], ACT.Exp).then_inc(exp_done, 1)

            def step(t, A, B, Cc):
                if A:
                    act.wait_ge(ctx2_in, t * 32 + 32)
                    if not (isinstance(t, int) and t == 0):
                        act.wait_ge(tr_ready, t * 4)
                    nc.scalar.activation(ca[0:C], ctx2[0:C], ACT.Copy).then_inc(ca_done, 1)
                    for b in range(2):
                        act.wait_ge(qk_ready, t * 2 + (b + 1))
                        if isinstance(t, int) and t == 0:
                            act.wait_ge(m_done, 2)
                        nc.scalar.activation(qa[:, b, :], (bank_a, bank_b)[b][0:Q1, :], ACT.Identity,
                                             bias=qk_bias[:]).then_inc(qa_done, 1)
                if isinstance(t, int) and t == 0:
                    act.wait_ge(w_small, 16 * (N_SMALL + 4))
                if B:
                    act.wait_ge(v1_ready, t)
                    nc.scalar.activation(v1[:], g6, ACT.Identity, bias=bv1_col[:]).then_inc(v1_done, 1)
                    act.wait_ge(xt_ready, t)
                    nc.scalar.activation(whole(xt_hi[:]), g7, ACT.Copy).then_inc(xt_hi_done, 1)
                    act.wait_ge(low_ready, t)
                    nc.scalar.activation(low[0:C, :], g6[0:C, 0:P], ACT.Copy).then_inc(low_done, 1)
                if Cc:
                    act.wait_ge(yt_ready, t - 1)
                    nc.scalar.activation(whole(yt_hi[:]), g6, ACT.Copy).then_inc(yt_hi_done, 1)
                if A:
                    for b in range(2):
                        for g in range(2):
                            exponentials(t, b, g)
                if B:
                    act.wait_ge(shift_done, t)
                    nc.scalar.activation(prob1[:], shifted[:], ACT.Exp, scale=float(E) ** -0.5).then_inc(p1_done, 1)
                    act.wait_ge(pt_ready, t)
                    pt = gen[0:E].rearrange("e g (h d) -> e (g h) d", d=P)
                    for b in range(2):
                        nc.scalar.activation(prob1t[C * b:C * b + C], pt[:, :, C * b:C * b + C],
                                             ACT.Copy).then_inc(pt_done, 1)
                if isinstance(t, int) and t == 0:
                    prepare_ffn0()
                    prepare_ffn1()

            run(act, before, step)

        @block.tensor
        def _(pe):
            mm = nc.tensor.matmul

            def before():
                pe.wait_ge(w_small, 16 * N_SMALL)
                mm(bank_a[:, 0:Q1], whole(wq_twice[:]), wk_bk[:], start=True, stop=True).then_inc(m_ready, 1)
                mm(bank_b[0:Q1, 0:1], wk_bk[:], bq0[:], start=True, stop=True).then_inc(m_ready, 1)
                pe.wait_ge(pool_const, 1)
                pe.wait_ge(dve_const, 1)
                for n in range(5):
                    last = nc.tensor.transpose(scores[0][:, n // 4, (n % 4) * P:(n % 4) * P + P], diag[:, n, :], ident[:])
                last.then_inc(diag_ready, 1)

            def prepare_ffn0():
                pe.wait_ge(w_lora, 16 * N_LORA)
                pe.wait_ge(pool_const, 2)
                for c in range(KC):
                    mm(g6[:, c * PAIRS:(c + 1) * PAIRS], sel_a[:, c].rearrange("n q r -> n (q r)"), gate_t[:],
                       start=True, stop=True)
                mm(g6[:, KC * PAIRS:5 * PAIRS], whole(sel_b[:]), gate_t[:], start=True, stop=True).then_inc(gate_ready, 1)
                pe.wait_ge(mix_done, 2)
                for k in range(KC):
                    if k >= 2:
                        pe.wait_ge(ae_lo_done, k - 1)
                    for c in range(KC):
                        last = mm(gen[:, k % 2, 0:PAIRS * R], lora_a[:, c, k * P:k * P + P],
                                  mix_a[:, c * PAIRS:(c + 1) * PAIRS, :].rearrange("p b r -> p (b r)"),
                                  start=(c == 0), stop=(c == KC - 1))
                    last.then_inc(ae_ready, 1)
                pe.wait_ge(ae_lo_done, 3)
                for k in range(KC):
                    last = nc.tensor.transpose(g6[:, k * R:k * R + R], share_a[:, k * P:k * P + P], ident[0:R, 0:R])
                last.then_inc(sh_ready, 1)
                pe.wait_ge(ae_lo_done, 4)
                for k in range(KC):
                    last = nc.tensor.transpose(g7[0:R, k * P:k * P + P], share_b[:, k, :], ident[:])
                last.then_inc(sh_ready, 1)
                pe.wait_ge(ae_lo_done, 5)
                pe.wait_ge(sh_done, 1)
                for o in range(C):
                    q, m = o % 4, o // 4
                    last = mm(gen[R * q:R * q + R, m // 8, (m % 8) * C:(m % 8) * C + C], lora_b[:, o, :],
                              whole(mix_b[:]), start=True, stop=True)
                last.then_inc(be_ready, 1)

            def prepare_ffn1():
                pe.wait_ge(w1_deq, KC)
                pe.wait_ge(be_done, 4)
                for k in range(KC):
                    if k >= 2:
                        pe.wait_ge(w1_lo_done, k - 1)
                    for o in range(KC):
                        last = nc.tensor.transpose(gen[:, k % 2, o * P:o * P + P], kern[:, o, k * P:k * P + P], ident[:])
                    last.then_inc(w1_ready, 1)

            def make_qk(t):
                pe.wait_ge(cb_lo_done, t + 1)
                pe.wait_ge(ca_done, t + 1)
                if isinstance(t, int) and t == 0:
                    pe.wait_ge(m_done, 3)
                else:
                    pe.wait_ge(att_done, t)
                for b in range(2):
                    to = (bank_a, bank_b)[b][0:Q1, :]
                    mm(to, m_hi[:], cb[:, b, :], start=True, stop=False)
                    mm(to, m_lo[:], ca[0:C, b, :], start=False, stop=True).then_inc(qk_ready, 1)

            def natural(t, b, g):
                pe.wait_ge(qa_done, t * 2 + (b + 1))
                if b == 0 and g == 0 and isinstance(t, int) and t == 0:
                    pe.wait_ge(diag_done, 5)
                elif b == 0 and not (isinstance(t, int) and t == 0):
                    pe.wait_ge(exp_done, t * 4 + (g - 1))
                elif b == 1:
                    pe.wait_ge(max_done, t * 4 + (g + 1))
                for j in range(2):
                    c = 2 * g + j
                    last = mm(scores[g][:, j, :], qa[:, b, c * P:c * P + P], ca[:, b, :], start=True, stop=True)
                last.then_inc(nat_ready, 1)

            def max_rows(t, b):
                pe.wait_ge(max_done, t * 4 + (2 * b + 2))
                if b == 0:
                    pe.wait_ge(qb_done, t * 4 + 4)
                else:
                    pe.wait_ge(row_done, t * 2 + 1)
                for c in range(KC):
                    last = nc.tensor.transpose(bank_b[0:1, c * P:c * P + P], neg_max[:, b, c:c + 1], ident[:])
                last.then_inc(row_ready, 1)

            def transposed(t, b, g):
                pe.wait_ge(row_done, t * 2 + (b + 1))
                pe.wait_ge(qb_done, t * 4 + (2 * b + 2))
                if b == 0:
                    pe.wait_ge(max_done, t * 4 + (g + 3))
                else:
                    pe.wait_ge(exp_done, t * 4 + (g + 1))
                for j in range(2):
                    c = 2 * g + j
                    mm(scores[g][:, j, :], ca[:, b, c * P:c * P + P], qa[:, b, :], start=True, stop=False)
                    last = mm(scores[g][:, j, :], cb[:, b, c * P:c * P + P], qb[:, b, :], start=False, stop=True)
                last.then_inc(tr_ready, 1)

            def make_v0(t):
                pe.wait_ge(ln_done[0], t + 1)
                pe.wait_ge(qb_done, t * 4 + 2)
                for c in range(KC):
                    last = mm(bank_a[:, c * P:c * P + P], norm[0][:, c * P:c * P + P], diag_t[:, V0, :],
                              start=True, stop=True)
                last.then_inc(v0_ready, 1)

            def numerator(t):
                pe.wait_ge(v0_done, t + 1)
                for c in range(KC):
                    if c % 2 == 0:
                        pe.wait_ge(exp_done, t * 4 + (3 + c // 2))
                    for b in range(2):
                        last = mm(bank_a[C * b:C * b + C, :], v0[:, c, C * b:C * b + C], prob[:, b, c, :],
                                  start=(c == 0), stop=(c == KC - 1))
                last.then_inc(num_ready, 1)

            def denominator(t):
                pe.wait_ge(sum_done, t * 2 + 2)
                for b in range(2):
                    last = mm(bank_b[C * b:C * b + C, :], ones[:], prob_sum[:, b, :], start=True, stop=True)
                last.then_inc(den_ready, 1)

            def make_k1(t):
                pe.wait_ge(ctx1_in, t * 16)
                if isinstance(t, int) and t == 1:
                    pe.wait_ge(w1_lo_done, KC)
                else:
                    pe.wait_ge(heads_done, t - 1)
                for c in range(KC):
                    last = mm(g6[:, c * P:c * P + P], ctx1[:, c * P:c * P + P], diag_t[:, WK, :], start=True, stop=True)
                last.then_inc(k1_ready, 1)

            def make_v1(t):
                pe.wait_ge(k1_done, t)
                mm(g6, diag_t[:, WV, :], ctx1[:], start=True, stop=True).then_inc(v1_ready, 1)

            def turn_x(t, Cc):
                pe.wait_ge(ln_done[1], t)
                if Cc:
                    pe.wait_ge(x3_done, t - 1)
                for c in range(KC):
                    last = nc.tensor.transpose(g7[:, c * P:c * P + P], norm[1][:, c * P:c * P + P], ident[:])
                last.then_inc(xt_ready, 1)

            def low_rank(t):
                pe.wait_ge(v1_done, t)
                pe.wait_ge(low_a_done, t * 2)
                pe.wait_ge(xt_lo_done, t)
                for c in range(KC):
                    for n, (w, x) in enumerate(((low_a_hi, xt_hi), (low_a_lo, xt_hi), (low_a_hi, xt_lo))):
                        last = mm(g6[0:Q1 + 1, 0:P], w[:, c, :], x[:, c, :], start=(c == 0 and n == 0),
                                  stop=(c == KC - 1 and n == 2))
                last.then_inc(low_ready, 1)

            def ffn0(t):
                for c in range(KC):
                    for n, (x, w) in enumerate(((xt_hi, kern_hi), (xt_hi, kern_lo), (xt_lo, kern_hi))):
                        mm(g7, x[:, c, :], w[:, c, :], start=(c == 0 and n == 0), stop=False)
                pe.wait_ge(low_done, t)
                mm(g7, low[:], low_b[:].rearrange("r b o -> r (b o)")[:, bass.ds((t - 1) * T, T)],
                   start=False, stop=True).then_inc(f0_ready, 1)

            def make_q1(t):
                pe.wait_ge(ln_done[2], t)
                for c in range(KC):
                    last = mm(g7[:, c * P:c * P + P], norm[2][:, c * P:c * P + P], diag_t[:, WQ, :], start=True, stop=True)
                last.then_inc(q1_ready, 1)

            def head_scores(t, Cc):
                pe.wait_ge(q1_done, t)
                if Cc:
                    pe.wait_ge(x4_done, t - 1)
                else:
                    pe.wait_ge(low_done, t)
                passed(pe)
                for h in range(H):
                    rows = slice(E * (h % 2), E * (h % 2) + E)
                    for b in range(2):
                        cols = slice(C * b, C * b + C)
                        last = mm(gen[cols, h % 2, (h // 2) * E:(h // 2) * E + E], q1t[rows, h // 2, cols],
                                  k1t[rows, h // 2, cols], start=True, stop=True)
                last.then_inc(s1_ready, 1)

            def turn_probs(t):
                pe.wait_ge(p1_done, t)
                passed(pe)
                for n in range(H):
                    last = nc.tensor.transpose(gen[0:E, n // 4, (n % 4) * P:(n % 4) * P + P], prob1[:, n, :], ident[:])
                last.then_inc(pt_ready, 1)

            def head_values(t):
                pe.wait_ge(pt_done, t * 2)
                passed(pe)
                for h in range(H):
                    n = (h % 2) * (H // 2) + h // 2
                    for b in range(2):
                        rows = slice(C * b, C * b + C)
                        last = mm(g6[rows, h * E:h * E + E], prob1t[rows, n, :], v1[rows, h * E:h * E + E],
                                  start=True, stop=True)
                last.then_inc(o1_ready, 1)

            def project(t):
                pe.wait_ge(heads_done, t - 1)
                mm(g7, diag_t[:, WO, :], heads[:], start=True, stop=True).then_inc(wo_ready, 1)

            def turn_y(t, B):
                pe.wait_ge(ln_done[3], t - 1)
                if B:
                    pe.wait_ge(low_done, t)
                for c in range(KC):
                    last = nc.tensor.transpose(g6[:, c * P:c * P + P], norm[3][:, c * P:c * P + P], ident[:])
                last.then_inc(yt_ready, 1)

            def ffn1(t):
                pe.wait_ge(yt_lo_done, t - 1)
                for c in range(KC):
                    for n, (x, w) in enumerate(((yt_hi, w1_hi), (yt_hi, w1_lo), (yt_lo, w1_hi))):
                        last = mm(g6, x[:, c, :], w[:, c, :], start=(c == 0 and n == 0), stop=(c == KC - 1 and n == 2))
                last.then_inc(f1_ready, 1)

            def step(t, A, B, Cc):
                if B:
                    make_k1(t)
                if Cc:
                    project(t)
                if A:
                    make_qk(t)
                if B:
                    make_v1(t)
                if A:
                    natural(t, 0, 0)
                    natural(t, 0, 1)
                if B:
                    turn_x(t, Cc)
                    low_rank(t)
                if A:
                    natural(t, 1, 0)
                    max_rows(t, 0)
                    natural(t, 1, 1)
                if Cc:
                    turn_y(t, B)
                if B:
                    ffn0(t)
                if A:
                    transposed(t, 0, 0)
                    max_rows(t, 1)
                    make_v0(t)
                    transposed(t, 0, 1)
                if Cc:
                    ffn1(t)
                if A:
                    transposed(t, 1, 0)
                if B:
                    make_q1(t)
                if A:
                    transposed(t, 1, 1)
                if B:
                    head_scores(t, Cc)
                if A:
                    numerator(t)
                if B:
                    turn_probs(t)
                if A:
                    denominator(t)
                if B:
                    head_values(t)
                if isinstance(t, int) and t == 0:
                    prepare_ffn0()
                    prepare_ffn1()

            run(pe, before, step)

        @block.vector
        def _(dve):
            v = nc.vector

            def ln_stats(i, src, count):
                v.bn_stats(stats[i][:], src[:]).then_inc(bn_done[i], 1)
                dve.wait_ge(bn_done[i], count)
                passed(dve)
                v.bn_aggr(mean_var[i][:], stats[i][:]).then_inc(mv_done[i], 1)

            def ln_apply(i, src, count):
                dve.wait_ge(rstd_done[i], count)
                v.tensor_scalar(norm[i][:], src[:], mean_var[i][:, 0:1], rstd[i][:], ALU.subtract,
                                ALU.mult).then_inc(ln_done[i], 1)

            def before():
                v.memset(diag[0:C, :, C:P], 0.0)
                v.memset(diag[C:P, :, 0:C], 0.0)
                v.memset(ca[C:Q1].bitcast(F32), 1.0)
                v.memset(low[C:Q1, :], 1.0).then_inc(dve_const, 1)
                dve.wait_ge(m_ready, 1)
                v.tensor_copy(m_hi[:], bank_a[:, 0:Q1]).then_inc(m_hi_done, 1)
                dve.wait_ge(m_ready, 2)
                v.tensor_copy(qk_bias[:], bank_b[0:Q1, 0:1]).then_inc(m_done, 1)
                dve.wait_ge(m_hi_done, 1)
                v.tensor_tensor(m_lo[:], bank_a[0:C, 0:Q1], m_hi[0:C, :].bitcast(F32), ALU.subtract).then_inc(m_done, 2)
                dve.wait_ge(tg_done, 1)
                dve.wait_ge(diag_ready, 1)
                for n in range(5):
                    src = scores[0][:, n // 4, (n % 4) * P:(n % 4) * P + P]
                    if n in (V0, WO):
                        v.tensor_scalar(diag_t[:, n, :], src, tg[:, (GX0 if n == V0 else GX1):][:, 0:1], None,
                                        ALU.mult).then_inc(diag_done, 1)
                    else:
                        v.tensor_copy(diag_t[:, n, :], src).then_inc(diag_done, 1)
                v.tensor_scalar(bv0_row[:], bv0_row[:], tg[:, GX0:GX0 + 1], None, ALU.mult).then_inc(row_bias_done, 1)

            def prepare_ffn0():
                dve.wait_ge(w_small, 16 * (N_SMALL + 4))
                v.tensor_scalar(bo_col[:], bo_col[:], tg[:, GX1:GX1 + 1], None, ALU.mult).then_inc(row_bias_done, 1)
                dve.wait_ge(pool_const, 2)
                v.tensor_reduce(eq_r[:], ident[:].rearrange("p (q r) -> p r q", q=4), AX.X, ALU.add).then_inc(gate_done, 1)
                v.tensor_reduce(eq_o[:], ident[:].rearrange("p (n o) -> p o n", n=NL), AX.X, ALU.add).then_inc(gate_done, 1)
                dve.wait_ge(gate_ready, 1)
                v.tensor_copy(gate_p[:], g6[:, 0:5 * PAIRS]).then_inc(gate_done, 1)
                dve.wait_ge(gate_done, 3)
                v.tensor_tensor(mix_a[:], gate_p[:, 0:KC * PAIRS].unsqueeze(2).broadcast_to([P, KC * PAIRS, R]),
                                eq_r[:].unsqueeze(1).broadcast_to([P, KC * PAIRS, R]), ALU.mult).then_inc(mix_done, 1)
                v.tensor_tensor(mix_b[:], gate_p[:, KC * PAIRS:].unsqueeze(2).broadcast_to([P, PAIRS, PAIRS]),
                                eq_o[:].unsqueeze(1).broadcast_to([P, PAIRS, PAIRS]), ALU.mult).then_inc(mix_done, 1)
                for k in range(KC):
                    dve.wait_ge(ae_hi_done, k + 1)
                    v.tensor_tensor(ae_lo[:, :, k, :], gen[:, k % 2, 0:PAIRS * R].rearrange("p (b r) -> p b r", b=PAIRS),
                                    ae_hi[:, :, k, :].bitcast(F32), ALU.subtract).then_inc(ae_lo_done, 1)
                dve.wait_ge(ae_hi_done, KC + 1)
                v.tensor_tensor(low_a_lo[:, :, R:2 * R], g6[:, 0:P].rearrange("p (k r) -> p k r", k=KC),
                                low_a_hi[:, :, R:2 * R].bitcast(F32), ALU.subtract).then_inc(ae_lo_done, 1)
                dve.wait_ge(sh_ready, 2)
                v.tensor_copy(share_bt[R:2 * R, :], g7[0:R, :]).then_inc(sh_done, 1)
                dve.wait_ge(sh_done, 1)
                v.tensor_copy(low_b[R:2 * R], share_bt[R:2 * R, :].unsqueeze(1).broadcast_to([R, PAIRS, T])).then_inc(low_b_done, 1)
                dve.wait_ge(be_ready, 1)
                for q in range(4):
                    v.tensor_copy(low_b[0:R].rearrange("r b (a m q) -> r (b a) m q", a=PAIRS, q=4)[:, :, :, q],
                                  gen[R * q:R * q + R].rearrange("r g (m x) -> r x (g m)", x=C)).then_inc(be_done, 1)
                dve.wait_ge(kern_hi_done, 1)
                v.tensor_tensor(kern_lo[:], kern[:], kern_hi[:].bitcast(F32), ALU.subtract).then_inc(kern_lo_done, 1)

            def prepare_ffn1():
                dve.wait_ge(w_ffn1, 16 * N_FFN1)
                dve.wait_ge(kern_lo_done, 1)
                for k in range(KC):
                    v.tensor_tensor(kern[:, k, :].rearrange("p (j i) -> p j i", i=QB_),
                                    q8[:, k, :].rearrange("p (j i) -> p j i", i=QB_),
                                    q_scale[:, k, :].unsqueeze(2).broadcast_to([P, T // QB_, QB_]), ALU.mult).then_inc(w1_deq, 1)
                v.tensor_scalar(b1_row[:], b1_row[:], tg[:, GF1:GF1 + 1], None, ALU.mult).then_inc(b1_done, 1)
                for k in range(KC):
                    dve.wait_ge(w1_hi_done, k + 1)
                    v.tensor_tensor(w1_lo[:, k, :], gen[:, k % 2, :], w1_hi[:, k, :].bitcast(F32),
                                    ALU.subtract).then_inc(w1_lo_done, 1)

            def maximum(t, b, g):
                dve.wait_ge(nat_ready, t * 4 + (2 * b + g + 1))
                v.tensor_reduce(neg_max[:, b, 2 * g:2 * g + 2], scores[g][:], AX.X, ALU.max,
                                negate=True).then_inc(max_done, 1)

            def shift_row(t, b):
                dve.wait_ge(row_ready, t * 2 + (b + 1))
                v.tensor_tensor(qa[C:Q1, b, :], bank_b[0:1, :], qa[C:Q1, b, :].bitcast(F32), ALU.add).then_inc(row_done, 1)

            def step(t, A, B, Cc):
                if B:
                    dve.wait_ge(x1_done, t)
                    ln_stats(1, x1, t)
                if A:
                    dve.wait_ge(ctx2_in, t * 32 + 32)
                    if not (isinstance(t, int) and t == 0):
                        dve.wait_ge(tr_ready, t * 4)
                    v.tensor_copy(cb[:], ctx2[:]).then_inc(cb_hi_done, 1)
                    dve.wait_ge(cb_hi_done, t + 1)
                    v.tensor_tensor(cb[C:P], ctx2[C:P], cb[C:P].bitcast(F32), ALU.subtract).then_inc(cb_lo_done, 1)
                if B:
                    ln_apply(1, x1, t)
                    dve.wait_ge(k1_ready, t)
                    v.tensor_tensor(k1t[:], g6.rearrange("p (k m) -> p k m", k=KC),
                                    whole(bk1_row[:]).unsqueeze(1).broadcast_to([P, KC, P]), ALU.add).then_inc(k1_done, 1)
                if Cc:
                    dve.wait_ge(wo_ready, t - 1)
                    v.scalar_tensor_tensor(out=x3[:], in0=g7, scalar=bo_col[:], in1=x2[:], op0=ALU.add,
                                           op1=ALU.add).then_inc(x3_done, 1)
                    dve.wait_ge(x3_done, t - 1)
                    ln_stats(3, x3, t - 1)
                if A:
                    for b in range(2):
                        dve.wait_ge(qa_done, t * 2 + (b + 1))
                        v.scalar_tensor_tensor(out=qb[0:C, b, :], in0=(bank_a, bank_b)[b][0:C, :], scalar=qk_bias[0:C, :],
                                               in1=qa[0:C, b, :].bitcast(F32), op0=ALU.add, op1=ALU.subtract).then_inc(qb_done, 1)
                        v.tensor_copy(qb[C:P, b, :], qa[0:C, b, :].bitcast(F32)).then_inc(qb_done, 1)
                if Cc:
                    ln_apply(3, x3, t - 1)
                if A:
                    maximum(t, 0, 0)
                if B:
                    dve.wait_ge(xt_hi_done, t)
                    v.tensor_tensor(whole(xt_lo[:]), g7, whole(xt_hi[:]).bitcast(F32), ALU.subtract).then_inc(xt_lo_done, 1)
                if A:
                    maximum(t, 0, 1)
                    dve.wait_ge(x_ln_in, t * 16 + 16)
                    ln_stats(0, x_ln, t + 1)
                    maximum(t, 1, 0)
                    shift_row(t, 0)
                    maximum(t, 1, 1)
                if Cc:
                    dve.wait_ge(yt_hi_done, t - 1)
                    v.tensor_tensor(whole(yt_lo[:]), g6, whole(yt_hi[:]).bitcast(F32), ALU.subtract).then_inc(yt_lo_done, 1)
                if A:
                    ln_apply(0, x_ln, t + 1)
                    shift_row(t, 1)
                if B:
                    dve.wait_ge(f0_ready, t)
                    v.scalar_tensor_tensor(out=x2[:], in0=g7, scalar=tg[:, GF0:GF0 + 1], in1=x1[:], op0=ALU.mult,
                                           op1=ALU.add).then_inc(x2_done, 1)
                    dve.wait_ge(x2_done, t)
                    ln_stats(2, x2, t)
                if A:
                    dve.wait_ge(v0_ready, t + 1)
                    if isinstance(t, int) and t == 0:
                        dve.wait_ge(row_bias_done, 1)
                    v.tensor_tensor(v0[:], bank_a[:].rearrange("p (k m) -> p k m", k=KC),
                                    whole(bv0_row[:]).unsqueeze(1).broadcast_to([P, KC, P]), ALU.add).then_inc(v0_done, 1)
                if B:
                    ln_apply(2, x2, t)
                if Cc:
                    dve.wait_ge(f1_ready, t - 1)
                    dve.wait_ge(x3b_done, t - 1)
                    dve.wait_ge(stored, t * 16 - 16)
                    v.scalar_tensor_tensor(out=x4[:], in0=g6, scalar=tg[:, GF1:GF1 + 1], in1=x3b[:], op0=ALU.mult,
                                           op1=ALU.add).then_inc(x4_done, 1)
                if B:
                    dve.wait_ge(q1_ready, t)
                    v.tensor_tensor(q1t[:], g7.rearrange("p (k m) -> p k m", k=KC),
                                    whole(bq1_row[:]).unsqueeze(1).broadcast_to([P, KC, P]), ALU.add).then_inc(q1_done, 1)
                    dve.wait_ge(s1_ready, t)
                    s1 = gen[:, :, 0:H // 2 * E].rearrange("p g (h e) -> p g h e", e=E)
                    v.tensor_reduce(head_max[:].rearrange("p (g h) -> p g h", g=2), s1, AX.X, ALU.max).then_inc(hmax_done, 1)
                    dve.wait_ge(hmax_done, t)
                    v.tensor_tensor(shifted[:].rearrange("p (g h) e -> p g h e", g=2), s1,
                                    head_max[:].rearrange("p (g h) -> p g h", g=2).unsqueeze(3).broadcast_to([P, 2, H // 2, E]),
                                    ALU.subtract).then_inc(shift_done, 1)
                    dve.wait_ge(p1_done, t)
                    v.tensor_reduce(head_sum[:], prob1[:], AX.X, ALU.add).then_inc(hsum_done, 1)
                    dve.wait_ge(hsum_done, t)
                    v.reciprocal(head_rec[:], head_sum[:]).then_inc(hrec_done, 1)
                if A:
                    dve.wait_ge(den_ready, t + 1)
                    v.reciprocal(recip[:], bank_b[:]).then_inc(recip_done, 1)
                    dve.wait_ge(recip_done, t + 1)
                    dve.wait_ge(num_ready, t + 1)
                    v.tensor_tensor(att[:], bank_a[:], recip[:], ALU.mult).then_inc(att_done, 1)
                    dve.wait_ge(att_done, t + 1)
                    dve.wait_ge(x_res_in, t * 16 + 16)
                    v.tensor_tensor(x1[:], att[:], x_res[:], ALU.add).then_inc(x1_done, 1)
                if B:
                    dve.wait_ge(o1_ready, t)
                    dve.wait_ge(hrec_done, t)
                    v.tensor_tensor(heads[:].rearrange("p (h g e) -> p h g e", g=2, e=E),
                                    g6.rearrange("p (h g e) -> p h g e", g=2, e=E),
                                    head_rec[:].rearrange("p (g h) -> p h g", g=2).unsqueeze(3).broadcast_to([P, H // 2, 2, E]),
                                    ALU.mult).then_inc(heads_done, 1)
                if isinstance(t, int) and t == 0:
                    prepare_ffn0()
                    prepare_ffn1()

            run(dve, before, step)

        @block.gpsimd
        def _(pool):
            g = nc.gpsimd

            def ln_rstd(i, count):
                pool.wait_ge(mv_done[i], count)
                passed(pool)
                g.tensor_scalar(var_eps[i][:], mean_var[i][:, 1:2], EPS, 1.0, ALU.add, ALU.mult).then_inc(eps_done[i], 1)
                pool.wait_ge(eps_done[i], count)
                g.tensor_tensor(rstd[i][:], var_eps[i][:], neg_half[:], ALU.pow).then_inc(rstd_done[i], 1)

            def before():
                g.memset(neg_half[:], -0.5)
                g.memset(ones[:], 1.0)
                g.memset(low_a_hi[:, :, 2 * R:].bitcast(F32), 0.0)
                g.memset(low_a_lo[:, :, 2 * R:].bitcast(F32), 0.0)
                g.memset(sel_a[:], 0.0).then_inc(pool_zero, 1)
                g.memset(sel_b[:], 0.0).then_inc(pool_zero, 1)
                g.memset(ident[:], 0.0).then_inc(pool_zero, 1)
                pool.wait_ge(pool_zero, 3)
                g.affine_select(out=ident[:], in_=ident[:], compare_op=ALU.not_equal, fill=1.0, base=0,
                                pattern=[[-1, P]], channel_multiplier=1).then_inc(pool_const, 1)
                g.affine_select(out=sel_a[:], in_=sel_a[:], compare_op=ALU.not_equal, fill=1.0, base=0,
                                pattern=[[-4, KC], [-1, 4], [0, R]], channel_multiplier=1)
                g.affine_select(out=sel_b[:], in_=sel_b[:], compare_op=ALU.not_equal, fill=1.0, base=0,
                                pattern=[[-1, NL], [0, PAIRS]], channel_multiplier=1).then_inc(pool_const, 1)

            def step(t, A, B, Cc):
                if B:
                    ln_rstd(1, t)
                if Cc:
                    ln_rstd(3, t - 1)
                if B:
                    if isinstance(t, int) and t == 1:
                        pool.wait_ge(ae_lo_done, 5)
                        pool.wait_ge(ae_hi_done, 5)
                    else:
                        pool.wait_ge(low_ready, t - 1)
                    for full, part in ((ae_hi, low_a_hi), (ae_lo, low_a_lo)):
                        g.tensor_copy(part[:, :, 0:R],
                                      full[:].rearrange("p b k r -> p (b k r)")[:, bass.ds((t - 1) * KC * R, KC * R)]
                                      .rearrange("p (k r) -> p k r", k=KC).bitcast(F32)).then_inc(low_a_done, 1)
                if Cc:
                    pool.wait_ge(x3_done, t - 1)
                    if isinstance(t, int) is False or t == 2:
                        pool.wait_ge(b1_done, 1)
                    g.tensor_tensor(x3b[:], x3[:], b1_row[:], ALU.add).then_inc(x3b_done, 1)
                if A:
                    ln_rstd(0, t + 1)
                if B:
                    ln_rstd(2, t)
                if A:
                    for b in range(2):
                        for k in range(2):
                            pool.wait_ge(exp_done, t * 4 + (2 * b + k + 1))
                            g.tensor_tensor(half[:, b, k, :], prob[:, b, 2 * k, :], prob[:, b, 2 * k + 1, :],
                                            ALU.add).then_inc(half_done, 1)
                        pool.wait_ge(half_done, t * 4 + (2 * b + 2))
                        g.tensor_tensor(prob_sum[:, b, :], half[:, b, 0, :], half[:, b, 1, :], ALU.add).then_inc(sum_done, 1)

            run(pool, before, step)


_INS = ["x", "ctx_4096", "g_xattn", "g_ffn", "L0_xattn_Wq", "L0_xattn_bq", "L0_xattn_Wk", "L0_xattn_bk",
        "L0_xattn_Wv", "L0_xattn_bv", "L0_ffn_gate", "L0_ffn_kernel", "L0_ffn_bias", "L0_ffn_lora_A",
        "L0_ffn_lora_B", "L0_ffn_lora_A_shared", "L0_ffn_lora_B_shared", "L1_xattn_Wq", "L1_xattn_bq",
        "L1_xattn_Wk", "L1_xattn_bk", "L1_xattn_Wv", "L1_xattn_bv", "L1_xattn_Wo", "L1_xattn_bo",
        "L1_ffn_quantized_weights", "L1_ffn_scale_values", "L1_ffn_bias"]


def kernel(**inputs):
    import numpy as _np
    import concourse.bacc as _bacc
    from concourse import mybir as _mybir
    from concourse.bass_utils import run_bass_kernel_spmd as _run

    nc = _bacc.Bacc("TRN2", target_bir_lowering=False, num_devices=1)
    arrays, args = {}, {}
    for name in _INS:
        arr = _np.ascontiguousarray(inputs[name])
        if arr.dtype == _np.int8:
            arr = arr.view(_np.int32)
        arrays[f"in_{name}"] = arr
        args[name] = nc.dram_tensor(f"in_{name}", arr.shape, _mybir.dt.from_np(arr.dtype), kind="ExternalInput").ap()
    out = nc.dram_tensor("out_x", (NB, C, T), _mybir.dt.float32, kind="ExternalOutput").ap()
    flamingo_two_layers(nc, args, out)
    r = _run(nc, [arrays], core_ids=[0])
    return r.results[0]["out_x"]
```

```python
from contextlib import ExitStack

import concourse.bass as bass
from concourse import mybir

F32 = mybir.dt.float32
F32R = mybir.dt.float32r
I8 = mybir.dt.int8
I32 = mybir.dt.int32
ALU = mybir.AluOpType
ACT = mybir.ActivationFunctionType
AX = mybir.AxisListType

P = 128
C = 64
T = 512
NB = 16
PAIRS = NB * C // P
KC = T // P
H = 8
E = T // H
NL, R = 16, 32
QB_ = 64
EPS = 1e-5
Q1 = C + 1


def flamingo_two_layers(nc, a, out):
    with ExitStack() as ctx:
        def sb(name, shape, dt=F32):
            return ctx.enter_context(nc.sbuf_tensor(name, shape, dt))

        def ps(name, shape):
            return ctx.enter_context(nc.psum_tensor(name, shape, F32))

        def sem(name):
            return ctx.enter_context(nc.semaphore(name))

        scores = [ps("scores0", [P, 2, T]), ps("scores1", [P, 2, T])]
        bank_a = ps("bank_a", [P, T])
        bank_b = ps("bank_b", [P, T])
        gen = ps("gen", [P, 2, T])
        g6, g7 = gen[:, 0, :], gen[:, 1, :]

        ident = sb("ident", [P, P])
        neg_half = sb("neg_half", [P, 1])
        gates = sb("gates", [P, 4])
        tg = sb("tg", [P, 4])
        GX0, GX1, GF0, GF1 = range(4)
        wq_twice = sb("wq_twice", [C, 2, C])
        wk_bk = sb("wk_bk", [C, Q1])
        bq0 = sb("bq0", [C, 1])
        m_hi = sb("m_hi", [P, Q1], F32R)
        m_lo = sb("m_lo", [C, Q1], F32R)
        qk_bias = sb("qk_bias", [Q1, 1])
        diag = sb("diag", [P, 5, P])
        diag_t = sb("diag_t", [P, 5, P])
        V0, WQ, WK, WV, WO = range(5)
        bv0_col = sb("bv0_col", [P, 1])
        bq1_row = sb("bq1_row", [P, 2, C])
        bk1_row = sb("bk1_row", [P, 2, C])
        bv1_col = sb("bv1_col", [P, 1])
        bo_col = sb("bo_col", [P, 1])
        kern = sb("kern", [P, KC, T])
        kern_hi = sb("kern_hi", [P, KC, T], F32R)
        kern_lo = sb("kern_lo", [P, KC, T], F32R)
        lora_a = sb("lora_a", [P, KC, T])
        lora_b = sb("lora_b", [P, C, R])
        share_a = sb("share_a", [R, T])
        share_b = sb("share_b", [P, KC, R])
        gate_t = sb("gate_t", [NL, PAIRS])
        sel_a = sb("sel_a", [NL, KC, 4, R])
        sel_b = sb("sel_b", [NL, NL, PAIRS])
        gate_p = sb("gate_p", [P, 5 * PAIRS])
        eq_r = sb("eq_r", [P, R])
        eq_o = sb("eq_o", [P, PAIRS])
        mix_a = sb("mix_a", [P, KC * PAIRS, R])
        mix_b = sb("mix_b", [P, PAIRS, PAIRS])
        ae_hi = sb("ae_hi", [P, PAIRS, KC, R], F32R)
        ae_lo = sb("ae_lo", [P, PAIRS, KC, R], F32R)
        low_a_hi = sb("low_a_hi", [P, KC, Q1 + 1], F32R)
        low_a_lo = sb("low_a_lo", [P, KC, Q1 + 1], F32R)
        low_b = sb("low_b", [Q1, PAIRS, T])
        share_bt = sb("share_bt", [2 * R, T])
        q_words = sb("q_words", [P, KC, T // 4], I32)
        q8 = q_words[:].rearrange("p k w -> p (k w)").bitcast(I8).rearrange("p (k i) -> p k i", k=KC)
        q_scale = sb("q_scale", [P, KC, T // QB_])
        w1_deq = sb("w1_deq", [P, KC, T])
        w1_hi = sb("w1_hi", [P, KC, T], F32R)
        w1_lo = sb("w1_lo", [P, KC, T], F32R)
        b1_row = sb("b1_row", [P, T])

        x_ln = sb("x_ln", [P, T])
        x_res = sb("x_res", [P, T])
        ctx2 = sb("ctx2", [P, 2, T])
        ca = sb("ca", [Q1, 2, T], F32R)
        cb = sb("cb", [P, 2, T], F32R)
        qa = sb("qa", [Q1, 2, T], F32R)
        qb = sb("qb", [P, 2, T], F32R)
        neg_max = sb("neg_max", [P, 2, KC])
        prob = sb("prob", [P, 2, KC, T])
        v0 = sb("v0", [P, KC, 2, Q1])
        recip = sb("recip", [P, KC, 2])
        att_t = sb("att_t", [P, KC, 2, C])
        x1 = sb("x1", [P, T])
        stats = [sb(f"stats{i}", [P, 6]) for i in range(4)]
        mean_var = [sb(f"mean_var{i}", [P, 2]) for i in range(4)]
        var_eps = [sb(f"var_eps{i}", [P, 1]) for i in range(4)]
        rstd = [sb(f"rstd{i}", [P, 1]) for i in range(4)]
        norm = [sb(f"norm{i}", [P, T]) for i in range(4)]
        ctx1 = sb("ctx1", [P, T])
        xt_hi = sb("xt_hi", [P, KC, P], F32R)
        xt_lo = sb("xt_lo", [P, KC, P], F32R)
        low = sb("low", [Q1, P])
        x2 = sb("x2", [P, T])
        k1t = sb("k1t", [P, KC, P])
        q1t = sb("q1t", [P, KC, P])
        v1 = sb("v1", [P, T])
        head_max = sb("head_max", [P, H])
        shifted = sb("shifted", [P, H, E])
        prob1 = sb("prob1", [P, H, E])
        head_sum = sb("head_sum", [P, H])
        head_rec = sb("head_rec", [P, H])
        prob1t = sb("prob1t", [P, H, E])
        heads = sb("heads", [P, T])
        x3 = sb("x3", [P, T])
        x3b = sb("x3b", [P, T])
        yt_hi = sb("yt_hi", [P, KC, P], F32R)
        yt_lo = sb("yt_lo", [P, KC, P], F32R)
        ffn1_gated = sb("ffn1_gated", [P, T])
        x4 = sb("x4", [P, T])

        w_m = sem("w_m")
        w_gates = sem("w_gates")
        w_v0 = sem("w_v0")
        w_attn1 = sem("w_attn1")
        w_lora_a = sem("w_lora_a")
        w_lora_b = sem("w_lora_b")
        w_ffn1 = sem("w_ffn1")
        w_kern = sem("w_kern")
        pool_const = sem("pool_const")
        dve_const = sem("dve_const")
        pool_zero = sem("pool_zero")
        tg_done = sem("tg_done")
        m_ready = sem("m_ready")
        m_done = sem("m_done")
        m_hi_done = sem("m_hi_done")
        diag_ready = sem("diag_ready")
        diag_done = sem("diag_done")
        row_bias_done = sem("row_bias_done")
        kern_hi_done = sem("kern_hi_done")
        kern_lo_done = sem("kern_lo_done")
        gate_ready = sem("gate_ready")
        gate_done = sem("gate_done")
        mix_done = sem("mix_done")
        ae_ready = sem("ae_ready")
        ae_hi_done = sem("ae_hi_done")
        ae_lo_done = sem("ae_lo_done")
        be_ready = sem("be_ready")
        be_done = sem("be_done")
        sh_ready = sem("sh_ready")
        sh_done = sem("sh_done")
        low_b_done = sem("low_b_done")
        w1_deq_done = sem("w1_deq_done")
        w1_ready = sem("w1_ready")
        w1_hi_done = sem("w1_hi_done")
        w1_lo_done = sem("w1_lo_done")
        b1_done = sem("b1_done")
        waits_passed = sem("waits_passed")
        x_ln_in = sem("x_ln_in")
        x_res_in = sem("x_res_in")
        ctx2_in = sem("ctx2_in")
        ctx1_in = sem("ctx1_in")
        stored = sem("stored")
        bn_done = [sem(f"bn_done{i}") for i in range(4)]
        mv_done = [sem(f"mv_done{i}") for i in range(4)]
        eps_done = [sem(f"eps_done{i}") for i in range(4)]
        rstd_done = [sem(f"rstd_done{i}") for i in range(4)]
        ln_done = [sem(f"ln_done{i}") for i in range(4)]
        ca_done = sem("ca_done")
        cb_hi_done = sem("cb_hi_done")
        cb_lo_done = sem("cb_lo_done")
        qk_ready = sem("qk_ready")
        qa_done = sem("qa_done")
        qb_hi_done = sem("qb_hi_done")
        qb_lo_done = sem("qb_lo_done")
        nat_ready = sem("nat_ready")
        max_done = sem("max_done")
        row_ready = sem("row_ready")
        row_done = sem("row_done")
        tr_ready = sem("tr_ready")
        exp_done = sem("exp_done")
        v0_ready = sem("v0_ready")
        v0_done = sem("v0_done")
        num_ready = sem("num_ready")
        recip_done = sem("recip_done")
        att_done = sem("att_done")
        att_turned = sem("att_turned")
        x1_done = sem("x1_done")
        k1_ready = sem("k1_ready")
        k1_done = sem("k1_done")
        pn_done = sem("pn_done")
        v1_ready = sem("v1_ready")
        v1_done = sem("v1_done")
        xt_ready = sem("xt_ready")
        xt_hi_done = sem("xt_hi_done")
        xt_lo_done = sem("xt_lo_done")
        low_a_done = sem("low_a_done")
        low_ready = sem("low_ready")
        low_done = sem("low_done")
        f0_ready = sem("f0_ready")
        x2_done = sem("x2_done")
        q1_ready = sem("q1_ready")
        q1_done = sem("q1_done")
        s1_ready = sem("s1_ready")
        hmax_done = sem("hmax_done")
        shift_done = sem("shift_done")
        p1_done = sem("p1_done")
        hsum_done = sem("hsum_done")
        hrec_done = sem("hrec_done")
        pt_ready = sem("pt_ready")
        pt_done = sem("pt_done")
        o1_ready = sem("o1_ready")
        heads_done = sem("heads_done")
        wo_ready = sem("wo_ready")
        x3_done = sem("x3_done")
        x3b_done = sem("x3b_done")
        yt_ready = sem("yt_ready")
        yt_hi_done = sem("yt_hi_done")
        yt_lo_done = sem("yt_lo_done")
        f1_ready = sem("f1_ready")
        gated_done = sem("gated_done")
        x4_done = sem("x4_done")

        N_M, N_GATES, N_V0, N_ATTN1, N_LORA_A, N_LORA_B, N_FFN1 = 5, 2, 4, 14, 3, 3, 3

        x_rows = a["x"].rearrange("b c t -> (b c) t")
        c_rows = a["ctx_4096"].rearrange("b c t -> (b c) t")
        o_rows = out.rearrange("b c t -> (b c) t")

        def rows_of(dram, p):
            return dram[bass.ds(p * P, P), :]

        def whole(ap):
            return ap.rearrange("p a b -> p (a b)")

        def tail_ffn1(p):
            return (scores[0][:, 0, :], scores[0][:, 1, :], scores[1][:, 0, :])[p - PAIRS + 3]

        block = ctx.enter_context(nc.Block())

        def passed(eng):
            eng.sem_inc(waits_passed, 1)

        def run(eng, before, step):
            before()
            step(0, True, False, False, False)
            step(1, True, True, False, False)
            step(2, True, True, True, False)
            with eng.Fori(3, PAIRS - 1) as t:
                step(t, True, True, True, True)
            step(PAIRS - 1, True, True, True, True, last=True)
            step(PAIRS, False, True, True, False)
            step(PAIRS + 1, False, False, True, False)

        @block.sync
        def _(sp):
            def load_ctx2(p):
                for k in range(2):
                    sp.dma_start(ctx2[C * k:C * k + C],
                                 rows_of(c_rows, p).rearrange("(b c) t -> c b t", b=2)).then_inc(ctx2_in, 16)

            def store(p):
                sp.wait_ge(x4_done, p + 1)
                sp.dma_start(rows_of(o_rows, p), x4[:]).then_inc(stored, 16)

            def before():
                sp.sem_inc(stored, 16)
                load_ctx2(0)
                sp.dma_start(x_ln[:], rows_of(x_rows, 0)).then_inc(x_ln_in, 16)
                sp.dma_start(gates[:, 0:2], a["g_xattn"].partition_broadcast(P)).then_inc(w_gates, 16)
                sp.dma_start(gates[:, 2:4], a["g_ffn"].partition_broadcast(P)).then_inc(w_gates, 16)
                for k in range(2):
                    half = slice(C * k, C * k + C)
                    sp.dma_start(diag[half, V0, half], a["L0_xattn_Wv"]).then_inc(w_v0, 16)
                    sp.dma_start(bv0_col[half, :], a["L0_xattn_bv"].unsqueeze(1)).then_inc(w_v0, 16)
                sp.dma_start(gate_t[:], a["L0_ffn_gate"].rearrange("b n -> n b"), allow_slow_non_contiguous=True).then_inc(w_lora_a, 16)
                sp.dma_start(lora_a[:], a["L0_ffn_lora_A"].rearrange("(c n) r i -> (n r) c i", n=4)).then_inc(w_lora_a, 16)
                sp.dma_start(share_a[:], a["L0_ffn_lora_A_shared"]).then_inc(w_lora_a, 16)
                for n, name in ((WK, "L1_xattn_Wk"), (WV, "L1_xattn_Wv"), (WQ, "L1_xattn_Wq"), (WO, "L1_xattn_Wo")):
                    for k in range(2):
                        half = slice(C * k, C * k + C)
                        sp.dma_start(diag[half, n, half], a[name]).then_inc(w_attn1, 16)
                for dst, name in ((bq1_row, "L1_xattn_bq"), (bk1_row, "L1_xattn_bk")):
                    sp.dma_start(dst[:], a[name].unsqueeze(0).unsqueeze(0).broadcast_to([P, 2, C])).then_inc(w_attn1, 16)
                for dst, name in ((bv1_col, "L1_xattn_bv"), (bo_col, "L1_xattn_bo")):
                    for k in range(2):
                        sp.dma_start(dst[C * k:C * k + C, :], a[name].unsqueeze(1)).then_inc(w_attn1, 16)
                sp.dma_start(x_res[:], rows_of(x_rows, 0)).then_inc(x_res_in, 16)
                sp.dma_start(q_words[:], a["L1_ffn_quantized_weights"].rearrange("(k p) i -> p k i", p=P)).then_inc(w_ffn1, 16)
                sp.dma_start(q_scale[:], a["L1_ffn_scale_values"].rearrange("(k p j) u -> p k (j u)", p=P, k=KC)).then_inc(w_ffn1, 16)
                sp.dma_start(b1_row[:], a["L1_ffn_bias"].partition_broadcast(P)).then_inc(w_ffn1, 16)
                sp.dma_start(share_b[:], a["L0_ffn_lora_B_shared"].rearrange("(k p) r -> p k r", p=P)).then_inc(w_lora_b, 16)
                sp.dma_start(lora_b[:], a["L0_ffn_lora_B"].rearrange("n (a o) r -> (n a) o r", a=PAIRS)).then_inc(w_lora_b, 16)
                sp.dma_start(low_b[C:Q1], a["L0_ffn_bias"].unsqueeze(0).unsqueeze(0).broadcast_to([1, PAIRS, T])).then_inc(w_lora_b, 16)
                sp.dma_start(kern[:], a["L0_ffn_kernel"].rearrange("(k p) o -> p k o", p=P)).then_inc(w_kern, 16)

            def step(t, A, B, Cc, D, last=False):
                if A:
                    if B:
                        sp.wait_ge(v1_ready, t)
                    sp.dma_start(ctx1[:], rows_of(c_rows, t)).then_inc(ctx1_in, 16)
                if A and not last:
                    sp.wait_ge(ln_done[0], t + 1)
                    sp.dma_start(x_ln[:], rows_of(x_rows, t + 1)).then_inc(x_ln_in, 16)
                if A and B:
                    sp.wait_ge(x1_done, t)
                    sp.dma_start(x_res[:], rows_of(x_rows, t)).then_inc(x_res_in, 16)
                if D:
                    store(t - 3)
                if B and not A:
                    store(PAIRS - 3)
                    store(PAIRS - 2)
                if Cc and not B:
                    store(PAIRS - 1)
                if A and not last:
                    sp.wait_ge(cb_lo_done, t + 1)
                    sp.wait_ge(ca_done, t + 1)
                    sp.wait_ge(cb_hi_done, t + 1)
                    load_ctx2(t + 1)

            run(sp, before, step)
            sp.wait_ge(stored, 16 * (PAIRS + 1))

        @block.scalar
        def _(act):
            def before():
                for k in range(2):
                    act.dma_start(wq_twice[:, k, :], a["L0_xattn_Wq"]).then_inc(w_m, 16)
                act.dma_start(wk_bk[:, 0:C], a["L0_xattn_Wk"]).then_inc(w_m, 16)
                act.dma_start(wk_bk[:, C:Q1], a["L0_xattn_bk"].unsqueeze(1)).then_inc(w_m, 16)
                act.dma_start(bq0[:], a["L0_xattn_bq"].unsqueeze(1)).then_inc(w_m, 16)
                split_ctx(0)
                act.wait_ge(w_gates, 16 * N_GATES)
                nc.scalar.activation(tg[:], gates[:], ACT.Tanh).then_inc(tg_done, 1)

            def effective_a(k):
                act.wait_ge(ae_ready, k + 1)
                nc.scalar.activation(ae_hi[:, :, k, :], gen[:, k % 2, 0:PAIRS * R].rearrange("p (b r) -> p b r", b=PAIRS),
                                     ACT.Copy).then_inc(ae_hi_done, 1)

            def shared_a():
                act.wait_ge(sh_ready, 1)
                nc.scalar.activation(low_a_hi[:, :, R:2 * R], g6[:, 0:P].rearrange("p (k r) -> p k r", k=KC),
                                     ACT.Copy).then_inc(ae_hi_done, 1)

            def turned_w1(k):
                act.wait_ge(w1_ready, k + 1)
                nc.scalar.activation(w1_hi[:, k, :], gen[:, k % 2, :], ACT.Copy).then_inc(w1_hi_done, 1)

            def effective_b(q):
                act.wait_ge(be_ready, 1)
                nc.scalar.activation(low_b[0:R].rearrange("r b (a m q) -> r (b a) m q", a=PAIRS, q=4)[:, :, :, q],
                                     gen[R * q:R * q + R].rearrange("r g (m x) -> r x (g m)", x=C),
                                     ACT.Copy).then_inc(be_done, 1)

            def split_ctx(p):
                act.wait_ge(ctx2_in, p * 32 + 32)
                if not (isinstance(p, int) and p == 0):
                    act.wait_ge(tr_ready, p * 4)
                nc.scalar.activation(cb[:], ctx2[:], ACT.Copy).then_inc(cb_hi_done, 1)
                nc.scalar.activation(ca[0:C], ctx2[0:C], ACT.Copy).then_inc(ca_done, 1)

            def exponentials(t, b, g):
                act.wait_ge(tr_ready, t * 4 + (2 * b + g + 1))
                nc.scalar.activation(prob[:, b, 2 * g:2 * g + 2, :], scores[g][:], ACT.Exp).then_inc(exp_done, 1)

            def step(t, A, B, Cc, D, last=False):
                first = isinstance(t, int) and t == 0
                if A:
                    for b in range(2):
                        act.wait_ge(qk_ready, t * 2 + (b + 1))
                        if isinstance(t, int) and t == 0:
                            act.wait_ge(m_done, 2)
                        nc.scalar.activation(qa[:, b, :], (bank_a, bank_b)[b][0:Q1, :], ACT.Identity,
                                             bias=qk_bias[:]).then_inc(qa_done, 1)
                if B:
                    act.wait_ge(xt_ready, t)
                    nc.scalar.activation(whole(xt_hi[:]), g6, ACT.Copy).then_inc(xt_hi_done, 1)
                if A:
                    for b in range(2):
                        act.wait_ge(qa_done, t * 2 + (b + 1))
                        nc.scalar.activation(qb[C:P, b, :], qa[0:C, b, :].bitcast(F32), ACT.Copy).then_inc(qb_hi_done, 1)
                if D:
                    act.wait_ge(f1_ready, t - 2)
                    nc.scalar.activation(ffn1_gated[:], g7, ACT.Copy, scale=tg[:, GF1:GF1 + 1]).then_inc(gated_done, 1)
                if B:
                    act.wait_ge(low_ready, t)
                    nc.scalar.activation(low[0:C, :], g7[0:C, 0:P], ACT.Copy).then_inc(low_done, 1)
                if first:
                    effective_a(0)
                if A:
                    exponentials(t, 0, 0)
                    act.wait_ge(v0_ready, t + 1)
                    nc.scalar.activation(v0[:, :, :, 0:C], bank_a[:].rearrange("p (k b c) -> p k b c", k=KC, b=2),
                                         ACT.Copy).then_inc(v0_done, 1)
                if first:
                    effective_a(1)
                if A:
                    exponentials(t, 0, 1)
                if Cc:
                    act.wait_ge(yt_ready, t - 1)
                    nc.scalar.activation(whole(yt_hi[:]), g7, ACT.Copy).then_inc(yt_hi_done, 1)
                if A:
                    exponentials(t, 1, 0)
                    exponentials(t, 1, 1)
                if first:
                    effective_a(2)
                    act.wait_ge(w_kern, 16)
                    nc.scalar.activation(kern_hi[:], kern[:], ACT.Copy).then_inc(kern_hi_done, 1)
                    effective_a(3)
                    shared_a()
                if A and not last:
                    split_ctx(t + 1)
                if B:
                    act.wait_ge(shift_done, t)
                    nc.scalar.activation(prob1[:], shifted[:], ACT.Exp, scale=float(E) ** -0.5).then_inc(p1_done, 1)
                    act.wait_ge(pt_ready, t)
                    pt = gen[0:E].rearrange("e g (h d) -> e (g h) d", d=P)
                    for b in range(2):
                        nc.scalar.activation(prob1t[C * b:C * b + C], pt[:, :, C * b:C * b + C],
                                             ACT.Copy).then_inc(pt_done, 1)
                    act.wait_ge(o1_ready, t)
                    nc.scalar.activation(heads[:], g6, ACT.Copy).then_inc(heads_done, 1)
                if A:
                    if first:
                        act.wait_ge(sh_done, 1)
                        nc.scalar.activation(low_b[R:2 * R, PAIRS // 2:],
                                             share_bt[R:2 * R, :].unsqueeze(1).broadcast_to([R, PAIRS // 2, T]),
                                             ACT.Copy).then_inc(low_b_done, 1)
                        effective_b(2)
                        effective_b(3)
                        act.wait_ge(w_attn1, 16 * N_ATTN1)
                    act.wait_ge(v1_ready, t + 1)
                    nc.scalar.activation(v1[:], scores[0][:, 1, :], ACT.Identity, bias=bv1_col[:]).then_inc(v1_done, 1)
                if first:
                    for k in range(KC):
                        turned_w1(k)

            run(act, before, step)

        @block.tensor
        def _(pe):
            mm = nc.tensor.matmul

            def before():
                pe.wait_ge(w_m, 16 * N_M)
                mm(bank_a[:, 0:Q1], whole(wq_twice[:]), wk_bk[:], start=True, stop=True).then_inc(m_ready, 1)
                mm(bank_b[0:Q1, 0:1], wk_bk[:], bq0[:], start=True, stop=True).then_inc(m_ready, 1)

            def gate_and_wv0():
                pe.wait_ge(w_lora_a, 16 * N_LORA_A)
                pe.wait_ge(pool_const, 2)
                for c in range(KC):
                    mm(g6[:, c * PAIRS:(c + 1) * PAIRS], sel_a[:, c].rearrange("n q r -> n (q r)"), gate_t[:],
                       start=True, stop=True)
                mm(g6[:, KC * PAIRS:5 * PAIRS], whole(sel_b[:]), gate_t[:], start=True, stop=True)
                pe.wait_ge(w_v0, 16 * N_V0)
                pe.wait_ge(dve_const, 1)
                nc.tensor.transpose(g6[:, P:2 * P], diag[:, V0, :], ident[:]).then_inc(gate_ready, 1)

            def turn_diag():
                pe.wait_ge(w_attn1, 16 * N_ATTN1)
                for n in (WQ, WK, WV, WO):
                    last = nc.tensor.transpose(g7[:, (n - 1) * P:n * P], diag[:, n, :], ident[:])
                last.then_inc(diag_ready, 1)

            def effective_a(k):
                if k == 0:
                    pe.wait_ge(mix_done, 2)
                    pe.wait_ge(diag_done, 1)
                elif k == 1:
                    pe.wait_ge(diag_done, 5)
                else:
                    pe.wait_ge(ae_lo_done, k - 1)
                for c in range(KC):
                    last = mm(gen[:, k % 2, 0:PAIRS * R], lora_a[:, c, k * P:k * P + P],
                              mix_a[:, c * PAIRS:(c + 1) * PAIRS, :].rearrange("p b r -> p (b r)"),
                              start=(c == 0), stop=(c == KC - 1))
                last.then_inc(ae_ready, 1)

            def shared():
                pe.wait_ge(ae_lo_done, 3)
                for k in range(KC):
                    last = nc.tensor.transpose(g6[:, k * R:k * R + R], share_a[:, k * P:k * P + P], ident[0:R, 0:R])
                last.then_inc(sh_ready, 1)
                pe.wait_ge(w_lora_b, 16 * N_LORA_B)
                pe.wait_ge(ae_lo_done, 4)
                for k in range(KC):
                    last = nc.tensor.transpose(g7[0:R, k * P:k * P + P], share_b[:, k, :], ident[:])
                last.then_inc(sh_ready, 1)

            def turn_w1(k):
                pe.wait_ge(w1_deq_done, KC)
                if k < 2:
                    pe.wait_ge(be_done, 4)
                else:
                    pe.wait_ge(w1_lo_done, k - 1)
                for o in range(KC):
                    last = nc.tensor.transpose(gen[:, k % 2, o * P:o * P + P], w1_deq[:, o, k * P:k * P + P], ident[:])
                last.then_inc(w1_ready, 1)

            def effective_b():
                pe.wait_ge(ae_lo_done, 5)
                pe.wait_ge(sh_done, 1)
                for o in range(C):
                    q, m = o % 4, o // 4
                    last = mm(gen[R * q:R * q + R, m // 8, (m % 8) * C:(m % 8) * C + C], lora_b[:, o, :],
                              whole(mix_b[:]), start=True, stop=True)
                last.then_inc(be_ready, 1)

            def make_qk(t):
                pe.wait_ge(cb_lo_done, t + 1)
                pe.wait_ge(ca_done, t + 1)
                if isinstance(t, int) and t == 0:
                    pe.wait_ge(m_done, 3)
                else:
                    pe.wait_ge(att_done, t * 2)
                for b in range(2):
                    to = (bank_a, bank_b)[b][0:Q1, :]
                    mm(to, m_hi[:], cb[:, b, :], start=True, stop=False)
                    mm(to, m_lo[:], ca[0:C, b, :], start=False, stop=True).then_inc(qk_ready, 1)

            def natural(t, b, g):
                pe.wait_ge(qa_done, t * 2 + (b + 1))
                if b == 0 and not (isinstance(t, int) and t == 0):
                    if g == 0:
                        pe.wait_ge(k1_done, t)
                        pe.wait_ge(v1_done, t)
                    else:
                        pe.wait_ge(x1_done, t)
                elif b == 1:
                    pe.wait_ge(max_done, t * 4 + (g + 1))
                for j in range(2):
                    c = 2 * g + j
                    last = mm(scores[g][:, j, :], qa[:, b, c * P:c * P + P], ca[:, b, :], start=True, stop=True)
                last.then_inc(nat_ready, 1)

            def max_rows(t, b):
                pe.wait_ge(max_done, t * 4 + (2 * b + 2))
                if b == 0:
                    pe.wait_ge(qb_lo_done, t * 2 + 2)
                else:
                    pe.wait_ge(row_done, t * 2 + 1)
                for c in range(KC):
                    last = nc.tensor.transpose(bank_b[0:1, c * P:c * P + P], neg_max[:, b, c:c + 1], ident[:])
                last.then_inc(row_ready, 1)

            def transposed(t, b, g):
                pe.wait_ge(row_done, t * 2 + (b + 1))
                pe.wait_ge(qb_lo_done, t * 2 + (b + 1))
                pe.wait_ge(qb_hi_done, t * 2 + (b + 1))
                if b == 0:
                    pe.wait_ge(max_done, t * 4 + (g + 3))
                else:
                    pe.wait_ge(exp_done, t * 4 + (g + 1))
                for j in range(2):
                    c = 2 * g + j
                    mm(scores[g][:, j, :], ca[:, b, c * P:c * P + P], qa[:, b, :], start=True, stop=False)
                    last = mm(scores[g][:, j, :], cb[:, b, c * P:c * P + P], qb[:, b, :], start=False, stop=True)
                last.then_inc(tr_ready, 1)

            def make_v0(t):
                pe.wait_ge(ln_done[0], t + 1)
                pe.wait_ge(qb_lo_done, t * 2 + 1)
                for c in range(KC):
                    last = mm(bank_a[:, c * P:c * P + P], norm[0][:, c * P:c * P + P], diag_t[:, V0, :],
                              start=True, stop=True)
                last.then_inc(v0_ready, 1)

            def values(t, b, s, chunks):
                pe.wait_ge(exp_done, t * 4 + (2 * b + s + 1))
                pe.wait_ge(v0_done, t + 1)
                pe.wait_ge(row_done, t * 2 + 2)
                for c in chunks:
                    at = ((c % 2) * 2 + b) * Q1
                    for k in (2 * s, 2 * s + 1):
                        last = mm((bank_a, bank_b)[c // 2][:, at:at + Q1], prob[:, b, k, c * P:c * P + P], v0[:, k, b, :],
                                  start=(b == 0 and k == 0 and c % 2 == 0),
                                  stop=(b == 1 and k == KC - 1 and c % 2 == 1))
                return last

            def turn_att(t):
                pe.wait_ge(exp_done, t * 4 + 4)
                for c in range(KC):
                    if c % 2 == 0:
                        pe.wait_ge(att_done, t * 2 + (1 + c // 2))
                    last = nc.tensor.transpose(scores[1][:, 0, c * P:c * P + P], att_t[:, c].rearrange("p b c -> p (b c)"),
                                               ident[:])
                last.then_inc(att_turned, 1)

            def make_k1(t):
                pe.wait_ge(ctx1_in, t * 16 + 16)
                pe.wait_ge(exp_done, t * 4 + 3)
                for c in range(KC):
                    last = mm(scores[0][:, 0, c * P:c * P + P], ctx1[:, c * P:c * P + P], diag_t[:, WK, :], start=True, stop=True)
                last.then_inc(k1_ready, 1)

            def make_v1(t):
                mm(scores[0][:, 1, :], diag_t[:, WV, :], ctx1[:], start=True, stop=True).then_inc(v1_ready, 1)

            def turn_x(t, Cc):
                pe.wait_ge(ln_done[1], t)
                if isinstance(t, int) and t == 1:
                    pe.wait_ge(w1_lo_done, KC)
                if Cc:
                    pe.wait_ge(heads_done, t - 1)
                for c in range(KC):
                    last = nc.tensor.transpose(g6[:, c * P:c * P + P], norm[1][:, c * P:c * P + P], ident[:])
                last.then_inc(xt_ready, 1)

            def low_rank(t, D):
                if D:
                    pe.wait_ge(gated_done, t - 2)
                pe.wait_ge(low_a_done, t * 2)
                pe.wait_ge(xt_lo_done, t)
                for c in range(KC):
                    for n, (w, x) in enumerate(((low_a_hi, xt_hi), (low_a_lo, xt_hi), (low_a_hi, xt_lo))):
                        last = mm(g7[0:Q1 + 1, 0:P], w[:, c, :], x[:, c, :], start=(c == 0 and n == 0),
                                  stop=(c == KC - 1 and n == 2))
                last.then_inc(low_ready, 1)

            def ffn0(t):
                if isinstance(t, int) and t == 1:
                    pe.wait_ge(kern_lo_done, 1)
                    pe.wait_ge(low_b_done, 2)
                for c in range(KC):
                    for n, (x, w) in enumerate(((xt_hi, kern_hi), (xt_hi, kern_lo), (xt_lo, kern_hi))):
                        mm(g6, x[:, c, :], w[:, c, :], start=(c == 0 and n == 0), stop=False)
                pe.wait_ge(low_done, t)
                mm(g6, low[:], low_b[:].rearrange("r b o -> r (b o)")[:, bass.ds((t - 1) * T, T)],
                   start=False, stop=True).then_inc(f0_ready, 1)

            def make_q1(t):
                pe.wait_ge(ln_done[2], t)
                for c in range(KC):
                    last = mm(g6[:, c * P:c * P + P], norm[2][:, c * P:c * P + P], diag_t[:, WQ, :], start=True, stop=True)
                last.then_inc(q1_ready, 1)

            def head_scores(t, Cc):
                pe.wait_ge(q1_done, t)
                if Cc:
                    pe.wait_ge(yt_lo_done, t - 1)
                else:
                    pe.wait_ge(low_done, t)
                passed(pe)
                for h in range(H):
                    rows = slice(E * (h % 2), E * (h % 2) + E)
                    for b in range(2):
                        cols = slice(C * b, C * b + C)
                        last = mm(gen[cols, h % 2, (h // 2) * E:(h // 2) * E + E], q1t[rows, h // 2, cols],
                                  k1t[rows, h // 2, cols], start=True, stop=True)
                last.then_inc(s1_ready, 1)

            def turn_probs(t):
                pe.wait_ge(pn_done, t)
                passed(pe)
                for n in range(H):
                    last = nc.tensor.transpose(gen[0:E, n // 4, (n % 4) * P:(n % 4) * P + P], prob1[:, n, :], ident[:])
                last.then_inc(pt_ready, 1)

            def head_values(t):
                pe.wait_ge(pt_done, t * 2)
                passed(pe)
                for h in range(H):
                    n = (h % 2) * (H // 2) + h // 2
                    for b in range(2):
                        rows = slice(C * b, C * b + C)
                        last = mm(g6[rows, h * E:h * E + E], prob1t[rows, n, :], v1[rows, h * E:h * E + E],
                                  start=True, stop=True)
                last.then_inc(o1_ready, 1)

            def project(t, bank):
                pe.wait_ge(heads_done, t - 1)
                mm(bank, diag_t[:, WO, :], heads[:], start=True, stop=True).then_inc(wo_ready, 1)

            def turn_y(t, A, B):
                pe.wait_ge(ln_done[3], t - 1)
                if B and not A:
                    pe.wait_ge(low_done, t)
                for c in range(KC):
                    last = nc.tensor.transpose(g7[:, c * P:c * P + P], norm[3][:, c * P:c * P + P], ident[:])
                last.then_inc(yt_ready, 1)

            def ffn1(p, bank, chunks):
                pe.wait_ge(yt_lo_done, p + 1)
                for c in chunks:
                    for n, (x, w) in enumerate(((yt_hi, w1_hi), (yt_hi, w1_lo), (yt_lo, w1_hi))):
                        last = mm(bank, x[:, c, :], w[:, c, :], start=(c == 0 and n == 0), stop=(c == KC - 1 and n == 2))
                return last

            def step(t, A, B, Cc, D, last=False):
                first = isinstance(t, int) and t == 0
                if A:
                    make_qk(t)
                if D:
                    ffn1(t - 3, g7, range(KC // 2))
                if B and not A:
                    pe.wait_ge(k1_done, PAIRS)
                    pe.wait_ge(v1_done, PAIRS)
                    ffn1(PAIRS - 3, tail_ffn1(PAIRS - 3), range(KC // 2))
                if B:
                    turn_x(t, Cc)
                if Cc and not A:
                    project(t, scores[1][:, 1, :])
                if A:
                    natural(t, 0, 0)
                if D:
                    ffn1(t - 3, g7, range(KC // 2, KC)).then_inc(f1_ready, 1)
                if A:
                    natural(t, 0, 1)
                if first:
                    gate_and_wv0()
                if B:
                    low_rank(t, D)
                if A:
                    natural(t, 1, 0)
                if Cc and A:
                    pe.wait_ge(low_done, t)
                    project(t, g7)
                if A:
                    max_rows(t, 0)
                    natural(t, 1, 1)
                if first:
                    effective_a(0)
                    turn_diag()
                if B:
                    ffn0(t)
                if B and not A:
                    ffn1(PAIRS - 3, tail_ffn1(PAIRS - 3), range(KC // 2, KC)).then_inc(f1_ready, 1)
                if A:
                    transposed(t, 0, 0)
                    max_rows(t, 1)
                    make_v0(t)
                if first:
                    effective_a(1)
                if A:
                    transposed(t, 0, 1)
                if Cc and not B:
                    ffn1(PAIRS - 2, tail_ffn1(PAIRS - 2), [3]).then_inc(f1_ready, 1)
                if Cc:
                    turn_y(t, A, B)
                if B:
                    make_q1(t)
                if A:
                    transposed(t, 1, 0)
                    values(t, 0, 0, range(KC))
                    transposed(t, 1, 1)
                if first:
                    effective_a(2)
                if B:
                    head_scores(t, Cc)
                if B and not A:
                    ffn1(PAIRS - 2, tail_ffn1(PAIRS - 2), [0, 1])
                if A:
                    values(t, 0, 1, range(KC))
                if first:
                    effective_a(3)
                if A:
                    values(t, 1, 0, range(KC))
                if first:
                    shared()
                if A:
                    values(t, 1, 1, range(KC)).then_inc(num_ready, 1)
                if first:
                    effective_b()
                if B:
                    turn_probs(t)
                if A:
                    make_k1(t)
                    turn_att(t)
                    make_v1(t)
                if B and not A:
                    ffn1(PAIRS - 2, tail_ffn1(PAIRS - 2), [2])
                if B:
                    head_values(t)
                if Cc and not B:
                    ffn1(PAIRS - 1, tail_ffn1(PAIRS - 1), range(KC)).then_inc(f1_ready, 1)
                if first:
                    for k in range(KC):
                        turn_w1(k)

            run(pe, before, step)

        @block.vector
        def _(dve):
            v = nc.vector

            def ln_stats(i, src, count):
                v.bn_stats(stats[i][:], src[:]).then_inc(bn_done[i], 1)
                dve.wait_ge(bn_done[i], count)
                passed(dve)
                v.bn_aggr(mean_var[i][:], stats[i][:]).then_inc(mv_done[i], 1)

            def ln_apply(i, src, count):
                dve.wait_ge(rstd_done[i], count)
                v.tensor_scalar(norm[i][:], src[:], mean_var[i][:, 0:1], rstd[i][:], ALU.subtract,
                                ALU.mult).then_inc(ln_done[i], 1)

            def split_ctx_low(p):
                dve.wait_ge(cb_hi_done, p + 1)
                v.tensor_tensor(cb[C:P], ctx2[C:P], cb[C:P].bitcast(F32), ALU.subtract).then_inc(cb_lo_done, 1)

            def before():
                v.memset(diag[0:C, :, C:P], 0.0)
                v.memset(diag[C:P, :, 0:C], 0.0)
                v.memset(ca[C:Q1].bitcast(F32), 1.0)
                v.memset(v0[:, :, :, C:Q1], 1.0)
                v.memset(low[C:Q1, :], 1.0).then_inc(dve_const, 1)
                dve.wait_ge(pool_const, 2)
                v.tensor_reduce(eq_r[:], ident[:].rearrange("p (q r) -> p r q", q=4), AX.X, ALU.add).then_inc(gate_done, 1)
                v.tensor_reduce(eq_o[:], ident[:].rearrange("p (n o) -> p o n", n=NL), AX.X, ALU.add).then_inc(gate_done, 1)
                dve.wait_ge(m_ready, 1)
                v.tensor_copy(m_hi[:], bank_a[:, 0:Q1]).then_inc(m_hi_done, 1)
                dve.wait_ge(m_ready, 2)
                v.tensor_copy(qk_bias[:], bank_b[0:Q1, 0:1]).then_inc(m_done, 1)
                dve.wait_ge(m_hi_done, 1)
                v.tensor_tensor(m_lo[:], bank_a[0:C, 0:Q1], m_hi[0:C, :].bitcast(F32), ALU.subtract).then_inc(m_done, 2)
                split_ctx_low(0)
                dve.wait_ge(x_ln_in, 16)
                ln_stats(0, x_ln, 1)
                ln_apply(0, x_ln, 1)

            def gate_and_wv0():
                dve.wait_ge(tg_done, 1)
                dve.wait_ge(gate_ready, 1)
                v.tensor_scalar(diag_t[:, V0, :], g6[:, P:2 * P], tg[:, GX0:GX0 + 1], None, ALU.mult).then_inc(diag_done, 1)
                v.tensor_scalar(bv0_col[:], bv0_col[:], tg[:, GX0:GX0 + 1], None, ALU.mult).then_inc(row_bias_done, 1)
                v.tensor_copy(gate_p[:], g6[:, 0:5 * PAIRS]).then_inc(gate_done, 1)
                dve.wait_ge(gate_done, 3)
                v.tensor_tensor(mix_a[:], gate_p[:, 0:KC * PAIRS].unsqueeze(2).broadcast_to([P, KC * PAIRS, R]),
                                eq_r[:].unsqueeze(1).broadcast_to([P, KC * PAIRS, R]), ALU.mult).then_inc(mix_done, 1)
                v.tensor_tensor(mix_b[:], gate_p[:, KC * PAIRS:].unsqueeze(2).broadcast_to([P, PAIRS, PAIRS]),
                                eq_o[:].unsqueeze(1).broadcast_to([P, PAIRS, PAIRS]), ALU.mult).then_inc(mix_done, 1)

            def turned_diag():
                dve.wait_ge(diag_ready, 1)
                for n in (WQ, WK, WV):
                    v.tensor_copy(diag_t[:, n, :], g7[:, (n - 1) * P:n * P]).then_inc(diag_done, 1)
                v.tensor_scalar(diag_t[:, WO, :], g7[:, (WO - 1) * P:WO * P], tg[:, GX1:GX1 + 1], None,
                                ALU.mult).then_inc(diag_done, 1)
                v.tensor_scalar(bo_col[:], bo_col[:], tg[:, GX1:GX1 + 1], None, ALU.mult).then_inc(row_bias_done, 1)

            def effective_a(k):
                dve.wait_ge(ae_hi_done, k + 1)
                v.tensor_tensor(ae_lo[:, :, k, :], gen[:, k % 2, 0:PAIRS * R].rearrange("p (b r) -> p b r", b=PAIRS),
                                ae_hi[:, :, k, :].bitcast(F32), ALU.subtract).then_inc(ae_lo_done, 1)

            def shared():
                dve.wait_ge(ae_hi_done, KC + 1)
                v.tensor_tensor(low_a_lo[:, :, R:2 * R], g6[:, 0:P].rearrange("p (k r) -> p k r", k=KC),
                                low_a_hi[:, :, R:2 * R].bitcast(F32), ALU.subtract).then_inc(ae_lo_done, 1)
                dve.wait_ge(sh_ready, 2)
                v.tensor_copy(share_bt[R:2 * R, :], g7[0:R, :]).then_inc(sh_done, 1)

            def spread_shared_b():
                dve.wait_ge(sh_done, 1)
                v.tensor_copy(low_b[R:2 * R, 0:PAIRS // 2],
                              share_bt[R:2 * R, :].unsqueeze(1).broadcast_to([R, PAIRS // 2, T])).then_inc(low_b_done, 1)

            def dequantise_w1():
                dve.wait_ge(w_ffn1, 16 * N_FFN1)
                for k in range(KC):
                    v.tensor_tensor(w1_deq[:, k, :].rearrange("p (j i) -> p j i", i=QB_),
                                    q8[:, k, :].rearrange("p (j i) -> p j i", i=QB_),
                                    q_scale[:, k, :].unsqueeze(2).broadcast_to([P, T // QB_, QB_]), ALU.mult).then_inc(w1_deq_done, 1)
                v.tensor_scalar(b1_row[:], b1_row[:], tg[:, GF1:GF1 + 1], None, ALU.mult).then_inc(b1_done, 1)

            def turned_w1(k):
                dve.wait_ge(w1_hi_done, k + 1)
                v.tensor_tensor(w1_lo[:, k, :], gen[:, k % 2, :], w1_hi[:, k, :].bitcast(F32),
                                ALU.subtract).then_inc(w1_lo_done, 1)

            def effective_b(q):
                dve.wait_ge(be_ready, 1)
                v.tensor_copy(low_b[0:R].rearrange("r b (a m q) -> r (b a) m q", a=PAIRS, q=4)[:, :, :, q],
                              gen[R * q:R * q + R].rearrange("r g (m x) -> r x (g m)", x=C)).then_inc(be_done, 1)

            def output_projected(t, bank, again):
                dve.wait_ge(wo_ready, t - 1)
                if again:
                    dve.wait_ge(x3b_done, t - 2)
                v.scalar_tensor_tensor(out=x3[:], in0=bank, scalar=bo_col[:], in1=x2[:], op0=ALU.add,
                                       op1=ALU.add).then_inc(x3_done, 1)

            def finish(p):
                dve.wait_ge(x3b_done, p + 1)
                dve.wait_ge(stored, 16 * (p + 1))
                dve.wait_ge(f1_ready, p + 1)
                v.scalar_tensor_tensor(out=x4[:], in0=tail_ffn1(p), scalar=tg[:, GF1:GF1 + 1], in1=x3b[:],
                                       op0=ALU.mult, op1=ALU.add).then_inc(x4_done, 1)

            def maximum(t, b, g):
                dve.wait_ge(nat_ready, t * 4 + (2 * b + g + 1))
                v.tensor_reduce(neg_max[:, b, 2 * g:2 * g + 2], scores[g][:], AX.X, ALU.max,
                                negate=True).then_inc(max_done, 1)

            def shift_row(t, b):
                dve.wait_ge(row_ready, t * 2 + (b + 1))
                v.tensor_tensor(qa[C:Q1, b, :], bank_b[0:1, :], qa[C:Q1, b, :].bitcast(F32), ALU.add).then_inc(row_done, 1)

            def step(t, A, B, Cc, D, last=False):
                first = isinstance(t, int) and t == 0
                if A:
                    for b in range(2):
                        dve.wait_ge(qa_done, t * 2 + (b + 1))
                        v.scalar_tensor_tensor(out=qb[0:C, b, :], in0=(bank_a, bank_b)[b][0:C, :], scalar=qk_bias[0:C, :],
                                               in1=qa[0:C, b, :].bitcast(F32), op0=ALU.add, op1=ALU.subtract).then_inc(qb_lo_done, 1)
                if B:
                    dve.wait_ge(xt_hi_done, t)
                    v.tensor_tensor(whole(xt_lo[:]), g6, whole(xt_hi[:]).bitcast(F32), ALU.subtract).then_inc(xt_lo_done, 1)
                if A:
                    maximum(t, 0, 0)
                    maximum(t, 0, 1)
                if first:
                    gate_and_wv0()
                if A:
                    maximum(t, 1, 0)
                    shift_row(t, 0)
                if Cc:
                    output_projected(t, g7 if A else scores[1][:, 1, :], D or not A)
                if A:
                    maximum(t, 1, 1)
                if first:
                    effective_a(0)
                    turned_diag()
                if Cc:
                    dve.wait_ge(x3_done, t - 1)
                    ln_stats(3, x3, t - 1)
                if B:
                    dve.wait_ge(f0_ready, t)
                    v.scalar_tensor_tensor(out=x2[:], in0=g6, scalar=tg[:, GF0:GF0 + 1], in1=x1[:], op0=ALU.mult,
                                           op1=ALU.add).then_inc(x2_done, 1)
                    dve.wait_ge(x2_done, t)
                    ln_stats(2, x2, t)
                if Cc and not B:
                    finish(PAIRS - 2)
                if Cc:
                    ln_apply(3, x3, t - 1)
                if A:
                    shift_row(t, 1)
                if first:
                    effective_a(1)
                if B:
                    ln_apply(2, x2, t)
                if B and not A:
                    finish(PAIRS - 3)
                if B:
                    dve.wait_ge(q1_ready, t)
                    v.tensor_tensor(q1t[:], g6.rearrange("p (k m) -> p k m", k=KC),
                                    whole(bq1_row[:]).unsqueeze(1).broadcast_to([P, KC, P]), ALU.add).then_inc(q1_done, 1)
                if Cc:
                    dve.wait_ge(yt_hi_done, t - 1)
                    v.tensor_tensor(whole(yt_lo[:]), g7, whole(yt_hi[:]).bitcast(F32), ALU.subtract).then_inc(yt_lo_done, 1)
                if A and not last:
                    dve.wait_ge(x_ln_in, t * 16 + 32)
                    ln_stats(0, x_ln, t + 2)
                if B:
                    dve.wait_ge(s1_ready, t)
                    s1 = gen[:, :, 0:H // 2 * E].rearrange("p g (h e) -> p g h e", e=E)
                    v.tensor_reduce(head_max[:].rearrange("p (g h) -> p g h", g=2), s1, AX.X, ALU.max).then_inc(hmax_done, 1)
                    dve.wait_ge(hmax_done, t)
                    v.tensor_tensor(shifted[:].rearrange("p (g h) e -> p g h e", g=2), s1,
                                    head_max[:].rearrange("p (g h) -> p g h", g=2).unsqueeze(3).broadcast_to([P, 2, H // 2, E]),
                                    ALU.subtract).then_inc(shift_done, 1)
                if A and not last:
                    dve.wait_ge(v0_ready, t + 1)
                    ln_apply(0, x_ln, t + 2)
                if first:
                    dequantise_w1()
                    effective_a(2)
                    effective_a(3)
                    shared()
                if A and not last:
                    split_ctx_low(t + 1)
                if B:
                    dve.wait_ge(p1_done, t)
                    v.tensor_reduce(head_sum[:], prob1[:], AX.X, ALU.add).then_inc(hsum_done, 1)
                    dve.wait_ge(hsum_done, t)
                    v.reciprocal(head_rec[:], head_sum[:]).then_inc(hrec_done, 1)
                    dve.wait_ge(hrec_done, t)
                    v.tensor_tensor(prob1[:], prob1[:], head_rec[:].unsqueeze(2).broadcast_to([P, H, E]),
                                    ALU.mult).then_inc(pn_done, 1)
                if Cc and not B:
                    finish(PAIRS - 1)
                if A:
                    dve.wait_ge(num_ready, t + 1)
                    prods = [bank[:, 0:4 * Q1].rearrange("p (k b c) -> p k b c", k=2, b=2) for bank in (bank_a, bank_b)]
                    for n in range(2):
                        v.reciprocal(recip[:, 2 * n:2 * n + 2], prods[n][:, :, :, C]).then_inc(recip_done, 1)
                    for n in range(2):
                        dve.wait_ge(recip_done, t * 2 + (n + 1))
                        v.tensor_tensor(att_t[:, 2 * n:2 * n + 2], prods[n][:, :, :, 0:C],
                                        recip[:, 2 * n:2 * n + 2].unsqueeze(3).broadcast_to([P, 2, 2, C]),
                                        ALU.mult).then_inc(att_done, 1)
                    if first:
                        spread_shared_b()
                        effective_b(0)
                        effective_b(1)
                    dve.wait_ge(att_turned, t + 1)
                    dve.wait_ge(x_res_in, t * 16 + 16)
                    if isinstance(t, int) and t == 0:
                        dve.wait_ge(row_bias_done, 1)
                    v.scalar_tensor_tensor(out=x1[:], in0=scores[1][:, 0, :], scalar=bv0_col[:], in1=x_res[:],
                                           op0=ALU.add, op1=ALU.add).then_inc(x1_done, 1)
                    dve.wait_ge(x1_done, t + 1)
                    ln_stats(1, x1, t + 1)
                    if first:
                        turned_w1(0)
                        turned_w1(1)
                    dve.wait_ge(k1_ready, t + 1)
                    v.tensor_tensor(k1t[:], scores[0][:, 0, :].rearrange("p (k m) -> p k m", k=KC),
                                    whole(bk1_row[:]).unsqueeze(1).broadcast_to([P, KC, P]), ALU.add).then_inc(k1_done, 1)
                    ln_apply(1, x1, t + 1)
                if first:
                    turned_w1(2)
                    turned_w1(3)

            run(dve, before, step)

        @block.gpsimd
        def _(pool):
            g = nc.gpsimd

            def ln_rstd(i, count):
                pool.wait_ge(mv_done[i], count)
                passed(pool)
                g.tensor_scalar(var_eps[i][:], mean_var[i][:, 1:2], EPS, 1.0, ALU.add, ALU.mult).then_inc(eps_done[i], 1)
                pool.wait_ge(eps_done[i], count)
                g.tensor_tensor(rstd[i][:], var_eps[i][:], neg_half[:], ALU.pow).then_inc(rstd_done[i], 1)

            def before():
                g.memset(neg_half[:], -0.5)
                g.memset(low_a_hi[:, :, 2 * R:].bitcast(F32), 0.0)
                g.memset(low_a_lo[:, :, 2 * R:].bitcast(F32), 0.0)
                g.memset(sel_a[:], 0.0).then_inc(pool_zero, 1)
                g.memset(sel_b[:], 0.0).then_inc(pool_zero, 1)
                g.memset(ident[:], 0.0).then_inc(pool_zero, 1)
                pool.wait_ge(pool_zero, 3)
                g.affine_select(out=ident[:], in_=ident[:], compare_op=ALU.not_equal, fill=1.0, base=0,
                                pattern=[[-1, P]], channel_multiplier=1).then_inc(pool_const, 1)
                g.affine_select(out=sel_a[:], in_=sel_a[:], compare_op=ALU.not_equal, fill=1.0, base=0,
                                pattern=[[-4, KC], [-1, 4], [0, R]], channel_multiplier=1)
                g.affine_select(out=sel_b[:], in_=sel_b[:], compare_op=ALU.not_equal, fill=1.0, base=0,
                                pattern=[[-1, NL], [0, PAIRS]], channel_multiplier=1).then_inc(pool_const, 1)
                ln_rstd(0, 1)

            def step(t, A, B, Cc, D, last=False):
                first = isinstance(t, int) and t == 0
                if B:
                    if isinstance(t, int) and t == 1:
                        pool.wait_ge(ae_lo_done, 5)
                        pool.wait_ge(ae_hi_done, 5)
                    else:
                        pool.wait_ge(low_ready, t - 1)
                    for full, part in ((ae_hi, low_a_hi), (ae_lo, low_a_lo)):
                        g.tensor_copy(part[:, :, 0:R],
                                      full[:].rearrange("p b k r -> p (b k r)")[:, bass.ds((t - 1) * KC * R, KC * R)]
                                      .rearrange("p (k r) -> p k r", k=KC).bitcast(F32)).then_inc(low_a_done, 1)
                if D:
                    pool.wait_ge(x3b_done, t - 2)
                    pool.wait_ge(gated_done, t - 2)
                    pool.wait_ge(stored, t * 16 - 32)
                    g.tensor_tensor(x4[:], ffn1_gated[:], x3b[:], ALU.add).then_inc(x4_done, 1)
                if Cc:
                    ln_rstd(3, t - 1)
                if B:
                    ln_rstd(2, t)
                if Cc:
                    if isinstance(t, int) and t == 2:
                        pool.wait_ge(b1_done, 1)
                    if not A:
                        pool.wait_ge(x4_done, t - 2)
                    g.tensor_tensor(x3b[:], x3[:], b1_row[:], ALU.add).then_inc(x3b_done, 1)
                if A and not last:
                    ln_rstd(0, t + 2)
                if first:
                    pool.wait_ge(kern_hi_done, 1)
                    g.tensor_tensor(kern_lo[:], kern[:], kern_hi[:].bitcast(F32), ALU.subtract).then_inc(kern_lo_done, 1)
                if A:
                    ln_rstd(1, t + 1)

            run(pool, before, step)


_INS = ["x", "ctx_4096", "g_xattn", "g_ffn", "L0_xattn_Wq", "L0_xattn_bq", "L0_xattn_Wk", "L0_xattn_bk",
        "L0_xattn_Wv", "L0_xattn_bv", "L0_ffn_gate", "L0_ffn_kernel", "L0_ffn_bias", "L0_ffn_lora_A",
        "L0_ffn_lora_B", "L0_ffn_lora_A_shared", "L0_ffn_lora_B_shared", "L1_xattn_Wq", "L1_xattn_bq",
        "L1_xattn_Wk", "L1_xattn_bk", "L1_xattn_Wv", "L1_xattn_bv", "L1_xattn_Wo", "L1_xattn_bo",
        "L1_ffn_quantized_weights", "L1_ffn_scale_values", "L1_ffn_bias"]


def kernel(**inputs):
    import numpy as _np
    import concourse.bacc as _bacc
    from concourse import mybir as _mybir
    from concourse.bass_utils import run_bass_kernel_spmd as _run

    nc = _bacc.Bacc("TRN2", target_bir_lowering=False, num_devices=1)
    arrays, args = {}, {}
    for name in _INS:
        arr = _np.ascontiguousarray(inputs[name])
        if arr.dtype == _np.int8:
            arr = arr.view(_np.int32)
        arrays[f"in_{name}"] = arr
        args[name] = nc.dram_tensor(f"in_{name}", arr.shape, _mybir.dt.from_np(arr.dtype), kind="ExternalInput").ap()
    out = nc.dram_tensor("out_x", (NB, C, T), _mybir.dt.float32, kind="ExternalOutput").ap()
    flamingo_two_layers(nc, args, out)
    r = _run(nc, [arrays], core_ids=[0])
    return r.results[0]["out_x"]
```

```python
from contextlib import ExitStack

import concourse.bass as bass
from concourse import mybir

F32 = mybir.dt.float32
F32R = mybir.dt.float32r
I8 = mybir.dt.int8
I32 = mybir.dt.int32
ALU = mybir.AluOpType
ACT = mybir.ActivationFunctionType
AX = mybir.AxisListType

P = 128
C = 64
T = 512
NB = 16
PAIRS = NB * C // P
KC = T // P
H = 8
E = T // H
NL, R = 16, 32
QB_ = 64
EPS = 1e-5
Q1 = C + 1


def flamingo_two_layers(nc, a, out):
    with ExitStack() as ctx:
        def sb(name, shape, dt=F32):
            return ctx.enter_context(nc.sbuf_tensor(name, shape, dt))

        def ps(name, shape):
            return ctx.enter_context(nc.psum_tensor(name, shape, F32))

        def sem(name):
            return ctx.enter_context(nc.semaphore(name))

        scores = [ps("scores0", [P, 2, T]), ps("scores1", [P, 2, T])]
        bank_a = ps("bank_a", [P, T])
        bank_b = ps("bank_b", [P, T])
        gen = ps("gen", [P, 2, T])
        g6, g7 = gen[:, 0, :], gen[:, 1, :]

        ident = sb("ident", [P, P])
        ones = sb("ones", [P, C])
        neg_half = sb("neg_half", [P, 1])
        gates = sb("gates", [P, 4])
        tg = sb("tg", [P, 4])
        GX0, GX1, GF0, GF1 = range(4)
        wq_twice = sb("wq_twice", [C, 2, C])
        wk_bk = sb("wk_bk", [C, Q1])
        bq0 = sb("bq0", [C, 1])
        m_hi = sb("m_hi", [P, Q1], F32R)
        m_lo = sb("m_lo", [C, Q1], F32R)
        qk_bias = sb("qk_bias", [Q1, 1])
        diag = sb("diag", [P, 5, P])
        diag_t = sb("diag_t", [P, 5, P])
        V0, WQ, WK, WV, WO = range(5)
        bv0_col = sb("bv0_col", [P, 1])
        bq1_row = sb("bq1_row", [P, 2, C])
        bk1_row = sb("bk1_row", [P, 2, C])
        bv1_col = sb("bv1_col", [P, 1])
        bo_col = sb("bo_col", [P, 1])
        kern = sb("kern", [P, KC, T])
        kern_hi = sb("kern_hi", [P, KC, T], F32R)
        kern_lo = sb("kern_lo", [P, KC, T], F32R)
        lora_a = sb("lora_a", [P, KC, T])
        lora_b = sb("lora_b", [P, C, R])
        share_a = sb("share_a", [R, T])
        share_b = sb("share_b", [P, KC, R])
        gate_t = sb("gate_t", [NL, PAIRS])
        sel_a = sb("sel_a", [NL, KC, 4, R])
        sel_b = sb("sel_b", [NL, NL, PAIRS])
        gate_p = sb("gate_p", [P, 5 * PAIRS])
        eq_r = sb("eq_r", [P, R])
        eq_o = sb("eq_o", [P, PAIRS])
        mix_a = sb("mix_a", [P, KC * PAIRS, R])
        mix_b = sb("mix_b", [P, PAIRS, PAIRS])
        ae_hi = sb("ae_hi", [P, PAIRS, KC, R], F32R)
        ae_lo = sb("ae_lo", [P, PAIRS, KC, R], F32R)
        low_a_hi = sb("low_a_hi", [P, KC, Q1 + 1], F32R)
        low_a_lo = sb("low_a_lo", [P, KC, Q1 + 1], F32R)
        low_b = sb("low_b", [Q1, PAIRS, T])
        share_bt = sb("share_bt", [2 * R, T])
        q_words = sb("q_words", [P, KC, T // 4], I32)
        q8 = q_words[:].rearrange("p k w -> p (k w)").bitcast(I8).rearrange("p (k i) -> p k i", k=KC)
        q_scale = sb("q_scale", [P, KC, T // QB_])
        late = sb("late", [P, KC, T])
        w1_deq = late
        w1_hi = sb("w1_hi", [P, KC, T], F32R)
        w1_lo = sb("w1_lo", [P, KC, T], F32R)
        b1_row = sb("b1_row", [P, T])

        x_ln = sb("x_ln", [P, T])
        x_res = sb("x_res", [P, T])
        ctx2 = sb("ctx2", [P, 2, T])
        ca = sb("ca", [Q1, 2, T], F32R)
        cb = sb("cb", [P, 2, T], F32R)
        qa = sb("qa", [Q1, 2, T], F32R)
        qb = sb("qb", [P, 2, T], F32R)
        neg_max = sb("neg_max", [P, 2, KC])
        prob = sb("prob", [P, 2, KC, T])
        half = sb("half", [P, 2, T])
        prob_sum = sb("prob_sum", [P, 2, T])
        v0 = sb("v0", [P, KC, P])
        numer = sb("numer", [P, T])
        denom = sb("denom", [P, T])
        recip = sb("recip", [P, T])
        att = numer
        x1 = sb("x1", [P, T])
        stats = [sb(f"stats{i}", [P, 6]) for i in range(4)]
        mean_var = [sb(f"mean_var{i}", [P, 2]) for i in range(4)]
        var_eps = [sb(f"var_eps{i}", [P, 1]) for i in range(4)]
        rstd = [sb(f"rstd{i}", [P, 1]) for i in range(4)]
        norm = [sb(f"norm{i}", [P, T]) for i in range(4)]
        ctx1 = sb("ctx1", [P, T])
        xt_hi = sb("xt_hi", [P, KC, P], F32R)
        xt_lo = sb("xt_lo", [P, KC, P], F32R)
        low = sb("low", [Q1, P])
        x2 = sb("x2", [P, T])
        k1t = sb("k1t", [P, KC, P])
        q1t = sb("q1t", [P, KC, P])
        v1 = sb("v1", [P, T])
        head_max = sb("head_max", [P, H])
        shifted = sb("shifted", [P, H, E])
        prob1 = sb("prob1", [P, H, E])
        head_sum = sb("head_sum", [P, H])
        head_rec = sb("head_rec", [P, H])
        prob1t = sb("prob1t", [P, H, E])
        heads = sb("heads", [P, T])
        x3 = late[:, 0, :]
        x3b = late[:, 1, :]
        yt_hi = sb("yt_hi", [P, KC, P], F32R)
        yt_lo = sb("yt_lo", [P, KC, P], F32R)
        ffn1_gated = late[:, 2, :]
        x4 = late[:, 3, :]

        w_m = sem("w_m")
        w_gates = sem("w_gates")
        w_v0 = sem("w_v0")
        w_attn1 = sem("w_attn1")
        w_lora_a = sem("w_lora_a")
        w_lora_b = sem("w_lora_b")
        w_ffn1 = sem("w_ffn1")
        w_kern = sem("w_kern")
        pool_const = sem("pool_const")
        dve_const = sem("dve_const")
        pool_zero = sem("pool_zero")
        tg_done = sem("tg_done")
        m_ready = sem("m_ready")
        m_done = sem("m_done")
        m_hi_done = sem("m_hi_done")
        diag_ready = sem("diag_ready")
        diag_done = sem("diag_done")
        row_bias_done = sem("row_bias_done")
        kern_hi_done = sem("kern_hi_done")
        kern_lo_done = sem("kern_lo_done")
        gate_ready = sem("gate_ready")
        gate_done = sem("gate_done")
        mix_done = sem("mix_done")
        ae_ready = sem("ae_ready")
        ae_hi_done = sem("ae_hi_done")
        ae_lo_done = sem("ae_lo_done")
        be_ready = sem("be_ready")
        be_done = sem("be_done")
        sh_ready = sem("sh_ready")
        sh_done = sem("sh_done")
        low_b_done = sem("low_b_done")
        w1_deq_done = sem("w1_deq_done")
        w1_ready = sem("w1_ready")
        w1_hi_done = sem("w1_hi_done")
        w1_lo_done = sem("w1_lo_done")
        b1_done = sem("b1_done")
        waits_passed = sem("waits_passed")
        x_ln_in = sem("x_ln_in")
        x_res_in = sem("x_res_in")
        ctx2_in = sem("ctx2_in")
        ctx1_in = sem("ctx1_in")
        stored = sem("stored")
        bn_done = [sem(f"bn_done{i}") for i in range(4)]
        mv_done = [sem(f"mv_done{i}") for i in range(4)]
        eps_done = [sem(f"eps_done{i}") for i in range(4)]
        rstd_done = [sem(f"rstd_done{i}") for i in range(4)]
        ln_done = [sem(f"ln_done{i}") for i in range(4)]
        ca_done = sem("ca_done")
        cb_hi_done = sem("cb_hi_done")
        cb_lo_done = sem("cb_lo_done")
        qk_ready = sem("qk_ready")
        qa_done = sem("qa_done")
        qb_hi_done = sem("qb_hi_done")
        qb_lo_done = sem("qb_lo_done")
        nat_ready = sem("nat_ready")
        max_done = sem("max_done")
        row_ready = sem("row_ready")
        row_done = sem("row_done")
        tr_ready = sem("tr_ready")
        exp_done = sem("exp_done")
        v0_ready = sem("v0_ready")
        v0_done = sem("v0_done")
        num_ready = sem("num_ready")
        numer_done = sem("numer_done")
        half_done = sem("half_done")
        last_half_done = sem("last_half_done")
        sum_done = sem("sum_done")
        den_ready = sem("den_ready")
        denom_done = sem("denom_done")
        recip_done = sem("recip_done")
        att_done = sem("att_done")
        x1_done = sem("x1_done")
        k1_ready = sem("k1_ready")
        k1_done = sem("k1_done")
        pn_done = sem("pn_done")
        v1_ready = sem("v1_ready")
        v1_done = sem("v1_done")
        xt_ready = sem("xt_ready")
        xt_hi_done = sem("xt_hi_done")
        xt_lo_done = sem("xt_lo_done")
        low_a_done = sem("low_a_done")
        low_ready = sem("low_ready")
        low_done = sem("low_done")
        f0_ready = sem("f0_ready")
        x2_done = sem("x2_done")
        q1_ready = sem("q1_ready")
        q1_done = sem("q1_done")
        s1_ready = sem("s1_ready")
        hmax_done = sem("hmax_done")
        shift_done = sem("shift_done")
        p1_done = sem("p1_done")
        hsum_done = sem("hsum_done")
        hrec_done = sem("hrec_done")
        pt_ready = sem("pt_ready")
        pt_done = sem("pt_done")
        o1_ready = sem("o1_ready")
        heads_done = sem("heads_done")
        wo_ready = sem("wo_ready")
        x3_done = sem("x3_done")
        x3b_done = sem("x3b_done")
        yt_ready = sem("yt_ready")
        yt_hi_done = sem("yt_hi_done")
        yt_lo_done = sem("yt_lo_done")
        f1_ready = sem("f1_ready")
        gated_done = sem("gated_done")
        x4_done = sem("x4_done")

        N_M, N_GATES, N_V0, N_ATTN1, N_LORA_A, N_LORA_B, N_FFN1 = 5, 2, 4, 14, 3, 3, 3

        x_rows = a["x"].rearrange("b c t -> (b c) t")
        c_rows = a["ctx_4096"].rearrange("b c t -> (b c) t")
        o_rows = out.rearrange("b c t -> (b c) t")

        def rows_of(dram, p):
            return dram[bass.ds(p * P, P), :]

        def whole(ap):
            return ap.rearrange("p a b -> p (a b)")

        def tail_ffn1(p):
            return (scores[1][:, 0, :], scores[0][:, 1, :], scores[0][:, 0, :])[p - PAIRS + 3]

        def ffn0_bank(A):
            return g7 if A else bank_a[:]

        def low_rank_bank(A):
            return g6 if A else g7

        block = ctx.enter_context(nc.Block())

        def passed(eng):
            eng.sem_inc(waits_passed, 1)

        def run(eng, before, step):
            before()
            step(0, True, False, False, False)
            step(1, True, True, False, False)
            step(2, True, True, True, False)
            with eng.Fori(3, PAIRS - 1) as t:
                step(t, True, True, True, True)
            step(PAIRS - 1, True, True, True, True, last=True)
            step(PAIRS, False, True, True, False)
            step(PAIRS + 1, False, False, True, False)

        @block.sync
        def _(sp):
            def load_ctx2(p):
                for k in range(2):
                    sp.dma_start(ctx2[C * k:C * k + C],
                                 rows_of(c_rows, p).rearrange("(b c) t -> c b t", b=2)).then_inc(ctx2_in, 16)

            def store(p):
                sp.wait_ge(x4_done, p + 1)
                sp.dma_start(rows_of(o_rows, p), x4[:]).then_inc(stored, 16)

            def before():
                sp.sem_inc(stored, 16)
                load_ctx2(0)
                sp.dma_start(x_ln[:], rows_of(x_rows, 0)).then_inc(x_ln_in, 16)
                sp.dma_start(gates[:, 0:2], a["g_xattn"].partition_broadcast(P)).then_inc(w_gates, 16)
                sp.dma_start(gates[:, 2:4], a["g_ffn"].partition_broadcast(P)).then_inc(w_gates, 16)
                for k in range(2):
                    half = slice(C * k, C * k + C)
                    sp.dma_start(diag[half, V0, half], a["L0_xattn_Wv"]).then_inc(w_v0, 16)
                    sp.dma_start(bv0_col[half, :], a["L0_xattn_bv"].unsqueeze(1)).then_inc(w_v0, 16)
                sp.dma_start(gate_t[:], a["L0_ffn_gate"].rearrange("b n -> n b"), allow_slow_non_contiguous=True).then_inc(w_lora_a, 16)
                sp.dma_start(lora_a[:], a["L0_ffn_lora_A"].rearrange("(c n) r i -> (n r) c i", n=4)).then_inc(w_lora_a, 16)
                sp.dma_start(share_a[:], a["L0_ffn_lora_A_shared"]).then_inc(w_lora_a, 16)
                for n, name in ((WK, "L1_xattn_Wk"), (WV, "L1_xattn_Wv"), (WQ, "L1_xattn_Wq"), (WO, "L1_xattn_Wo")):
                    for k in range(2):
                        half = slice(C * k, C * k + C)
                        sp.dma_start(diag[half, n, half], a[name]).then_inc(w_attn1, 16)
                for dst, name in ((bq1_row, "L1_xattn_bq"), (bk1_row, "L1_xattn_bk")):
                    sp.dma_start(dst[:], a[name].unsqueeze(0).unsqueeze(0).broadcast_to([P, 2, C])).then_inc(w_attn1, 16)
                for dst, name in ((bv1_col, "L1_xattn_bv"), (bo_col, "L1_xattn_bo")):
                    for k in range(2):
                        sp.dma_start(dst[C * k:C * k + C, :], a[name].unsqueeze(1)).then_inc(w_attn1, 16)
                sp.dma_start(x_res[:], rows_of(x_rows, 0)).then_inc(x_res_in, 16)
                sp.dma_start(q_words[:], a["L1_ffn_quantized_weights"].rearrange("(k p) i -> p k i", p=P)).then_inc(w_ffn1, 16)
                sp.dma_start(q_scale[:], a["L1_ffn_scale_values"].rearrange("(k p j) u -> p k (j u)", p=P, k=KC)).then_inc(w_ffn1, 16)
                sp.dma_start(b1_row[:], a["L1_ffn_bias"].partition_broadcast(P)).then_inc(w_ffn1, 16)
                sp.dma_start(share_b[:], a["L0_ffn_lora_B_shared"].rearrange("(k p) r -> p k r", p=P)).then_inc(w_lora_b, 16)
                sp.dma_start(lora_b[:], a["L0_ffn_lora_B"].rearrange("n (a o) r -> (n a) o r", a=PAIRS)).then_inc(w_lora_b, 16)
                sp.dma_start(low_b[C:Q1], a["L0_ffn_bias"].unsqueeze(0).unsqueeze(0).broadcast_to([1, PAIRS, T])).then_inc(w_lora_b, 16)
                sp.dma_start(kern[:], a["L0_ffn_kernel"].rearrange("(k p) o -> p k o", p=P)).then_inc(w_kern, 16)

            def step(t, A, B, Cc, D, last=False):
                if A:
                    if B:
                        sp.wait_ge(v1_ready, t)
                    sp.dma_start(ctx1[:], rows_of(c_rows, t)).then_inc(ctx1_in, 16)
                if A and not last:
                    sp.wait_ge(ln_done[0], t + 1)
                    sp.dma_start(x_ln[:], rows_of(x_rows, t + 1)).then_inc(x_ln_in, 16)
                if A and B:
                    sp.wait_ge(x1_done, t)
                    sp.dma_start(x_res[:], rows_of(x_rows, t)).then_inc(x_res_in, 16)
                if D:
                    store(t - 3)
                if B and not A:
                    store(PAIRS - 3)
                    store(PAIRS - 2)
                if Cc and not B:
                    store(PAIRS - 1)
                if A and not last:
                    sp.wait_ge(cb_lo_done, t + 1)
                    sp.wait_ge(ca_done, t + 1)
                    sp.wait_ge(cb_hi_done, t + 1)
                    load_ctx2(t + 1)

            run(sp, before, step)
            sp.wait_ge(stored, 16 * (PAIRS + 1))

        @block.scalar
        def _(act):
            def before():
                for k in range(2):
                    act.dma_start(wq_twice[:, k, :], a["L0_xattn_Wq"]).then_inc(w_m, 16)
                act.dma_start(wk_bk[:, 0:C], a["L0_xattn_Wk"]).then_inc(w_m, 16)
                act.dma_start(wk_bk[:, C:Q1], a["L0_xattn_bk"].unsqueeze(1)).then_inc(w_m, 16)
                act.dma_start(bq0[:], a["L0_xattn_bq"].unsqueeze(1)).then_inc(w_m, 16)
                split_ctx_b(0)
                split_ctx_a(0)
                act.wait_ge(w_gates, 16 * N_GATES)
                nc.scalar.activation(tg[:], gates[:], ACT.Tanh).then_inc(tg_done, 1)

            def effective_a(k):
                act.wait_ge(ae_ready, k + 1)
                nc.scalar.activation(ae_hi[:, :, k, :], gen[:, k % 2, 0:PAIRS * R].rearrange("p (b r) -> p b r", b=PAIRS),
                                     ACT.Copy).then_inc(ae_hi_done, 1)

            def shared_a():
                act.wait_ge(sh_ready, 1)
                nc.scalar.activation(low_a_hi[:, :, R:2 * R], g6[:, 0:P].rearrange("p (k r) -> p k r", k=KC),
                                     ACT.Copy).then_inc(ae_hi_done, 1)

            def turned_w1(k):
                act.wait_ge(w1_ready, k + 1)
                nc.scalar.activation(w1_hi[:, k, :], scores[1][:, k % 2, :], ACT.Copy).then_inc(w1_hi_done, 1)

            def effective_b(q):
                act.wait_ge(be_ready, 1)
                nc.scalar.activation(low_b[0:R].rearrange("r b (a m q) -> r (b a) m q", a=PAIRS, q=4)[:, :, :, q],
                                     gen[R * q:R * q + R].rearrange("r g (m x) -> r x (g m)", x=C),
                                     ACT.Copy).then_inc(be_done, 1)

            def take_denominator(t):
                act.wait_ge(den_ready, t + 1)
                nc.scalar.activation(denom[:], bank_b[:], ACT.Copy).then_inc(denom_done, 1)

            def split_ctx_b(p):
                act.wait_ge(ctx2_in, p * 32 + 32)
                if not (isinstance(p, int) and p == 0):
                    act.wait_ge(tr_ready, p * 4)
                nc.scalar.activation(cb[:], ctx2[:], ACT.Copy).then_inc(cb_hi_done, 1)

            def split_ctx_a(p):
                nc.scalar.activation(ca[0:C], ctx2[0:C], ACT.Copy).then_inc(ca_done, 1)

            def exponentials(t, b, g):
                act.wait_ge(tr_ready, t * 4 + (2 * b + g + 1))
                nc.scalar.activation(prob[:, b, 2 * g:2 * g + 2, :], scores[g][:], ACT.Exp).then_inc(exp_done, 1)

            def step(t, A, B, Cc, D, last=False):
                first = isinstance(t, int) and t == 0
                if A:
                    for b in range(2):
                        act.wait_ge(qk_ready, t * 2 + (b + 1))
                        if isinstance(t, int) and t == 0:
                            act.wait_ge(m_done, 2)
                        nc.scalar.activation(qa[:, b, :], (bank_a, bank_b)[b][0:Q1, :], ACT.Identity,
                                             bias=qk_bias[:]).then_inc(qa_done, 1)
                if B:
                    act.wait_ge(xt_ready, t)
                    nc.scalar.activation(whole(xt_hi[:]), g6, ACT.Copy).then_inc(xt_hi_done, 1)
                if D:
                    act.wait_ge(f1_ready, t - 2)
                    nc.scalar.activation(ffn1_gated[:], g7, ACT.Copy, scale=tg[:, GF1:GF1 + 1]).then_inc(gated_done, 1)
                if A:
                    for b in range(2):
                        act.wait_ge(qa_done, t * 2 + (b + 1))
                        nc.scalar.activation(qb[0:C, b, :], qa[0:C, b, :].bitcast(F32), ACT.Copy).then_inc(qb_hi_done, 1)
                if isinstance(t, int) and t == 1:
                    act.wait_ge(sh_done, 1)
                    nc.scalar.activation(low_b[R:2 * R, PAIRS // 2:],
                                         share_bt[R:2 * R, :].unsqueeze(1).broadcast_to([R, PAIRS // 2, T]),
                                         ACT.Copy).then_inc(low_b_done, 1)
                if B:
                    act.wait_ge(low_ready, t)
                    nc.scalar.activation(low[0:C, :], low_rank_bank(A)[0:C, 0:P], ACT.Copy).then_inc(low_done, 1)
                if first:
                    effective_a(0)
                if A:
                    exponentials(t, 0, 0)
                    act.wait_ge(v0_ready, t + 1)
                    nc.scalar.activation(whole(v0[:]), bank_a[:], ACT.Copy).then_inc(v0_done, 1)
                if first:
                    effective_a(1)
                if A:
                    exponentials(t, 0, 1)
                if Cc:
                    act.wait_ge(yt_ready, t - 1)
                    nc.scalar.activation(whole(yt_hi[:]), g7, ACT.Copy).then_inc(yt_hi_done, 1)
                if A:
                    exponentials(t, 1, 0)
                    exponentials(t, 1, 1)
                if first:
                    effective_a(2)
                    act.wait_ge(w_kern, 16)
                    nc.scalar.activation(kern_hi[:], kern[:], ACT.Copy).then_inc(kern_hi_done, 1)
                    turned_w1(0)
                    turned_w1(1)
                    effective_a(3)
                    take_denominator(t)
                    shared_a()
                    act.wait_ge(num_ready, t + 1)
                    nc.scalar.activation(numer[:], bank_a[:], ACT.Copy).then_inc(numer_done, 1)
                    turned_w1(2)
                    turned_w1(3)
                if A and not last:
                    split_ctx_b(t + 1)
                if B:
                    act.wait_ge(shift_done, t)
                    nc.scalar.activation(prob1[:], shifted[:], ACT.Exp, scale=float(E) ** -0.5).then_inc(p1_done, 1)
                if A:
                    if not first:
                        take_denominator(t)
                    if not last:
                        split_ctx_a(t + 1)
                if B:
                    act.wait_ge(pt_ready, t)
                    pt = gen[0:E].rearrange("e g (h d) -> e (g h) d", d=P)
                    for b in range(2):
                        nc.scalar.activation(prob1t[C * b:C * b + C], pt[:, :, C * b:C * b + C],
                                             ACT.Copy).then_inc(pt_done, 1)
                if A and not first:
                    act.wait_ge(num_ready, t + 1)
                    nc.scalar.activation(numer[:], bank_a[:], ACT.Copy).then_inc(numer_done, 1)
                if B:
                    act.wait_ge(o1_ready, t)
                    nc.scalar.activation(heads[:], g6, ACT.Copy).then_inc(heads_done, 1)
                if A:
                    if first:
                        effective_b(1)
                        effective_b(2)
                        effective_b(3)
                        act.wait_ge(w_attn1, 16 * N_ATTN1)
                    act.wait_ge(v1_ready, t + 1)
                    nc.scalar.activation(v1[:], scores[0][:, 1, :], ACT.Identity, bias=bv1_col[:]).then_inc(v1_done, 1)

            run(act, before, step)

        @block.tensor
        def _(pe):
            mm = nc.tensor.matmul

            def before():
                pe.wait_ge(w_m, 16 * N_M)
                mm(bank_a[:, 0:Q1], whole(wq_twice[:]), wk_bk[:], start=True, stop=True).then_inc(m_ready, 1)
                mm(bank_b[0:Q1, 0:1], wk_bk[:], bq0[:], start=True, stop=True).then_inc(m_ready, 1)

            def gate_and_wv0():
                pe.wait_ge(w_lora_a, 16 * N_LORA_A)
                pe.wait_ge(pool_const, 2)
                for c in range(KC):
                    mm(g6[:, c * PAIRS:(c + 1) * PAIRS], sel_a[:, c].rearrange("n q r -> n (q r)"), gate_t[:],
                       start=True, stop=True)
                mm(g6[:, KC * PAIRS:5 * PAIRS], whole(sel_b[:]), gate_t[:], start=True, stop=True)
                pe.wait_ge(w_v0, 16 * N_V0)
                pe.wait_ge(dve_const, 1)
                nc.tensor.transpose(g6[:, P:2 * P], diag[:, V0, :], ident[:]).then_inc(gate_ready, 1)

            def turn_diag():
                pe.wait_ge(w_attn1, 16 * N_ATTN1)
                for n in (WQ, WK, WV, WO):
                    last = nc.tensor.transpose(g7[:, (n - 1) * P:n * P], diag[:, n, :], ident[:])
                last.then_inc(diag_ready, 1)

            def effective_a(k):
                if k == 0:
                    pe.wait_ge(mix_done, 2)
                    pe.wait_ge(diag_done, 1)
                elif k == 1:
                    pe.wait_ge(diag_done, 5)
                else:
                    pe.wait_ge(ae_lo_done, k - 1)
                for c in range(KC):
                    last = mm(gen[:, k % 2, 0:PAIRS * R], lora_a[:, c, k * P:k * P + P],
                              mix_a[:, c * PAIRS:(c + 1) * PAIRS, :].rearrange("p b r -> p (b r)"),
                              start=(c == 0), stop=(c == KC - 1))
                last.then_inc(ae_ready, 1)

            def shared():
                pe.wait_ge(ae_lo_done, 3)
                for k in range(KC):
                    last = nc.tensor.transpose(g6[:, k * R:k * R + R], share_a[:, k * P:k * P + P], ident[0:R, 0:R])
                last.then_inc(sh_ready, 1)
                pe.wait_ge(w_lora_b, 16 * N_LORA_B)
                pe.wait_ge(ae_lo_done, 4)
                for k in range(KC):
                    last = nc.tensor.transpose(g7[0:R, k * P:k * P + P], share_b[:, k, :], ident[:])
                last.then_inc(sh_ready, 1)

            def turn_w1(k):
                pe.wait_ge(w1_deq_done, KC)
                if k < 2:
                    pe.wait_ge(exp_done, 4)
                else:
                    pe.wait_ge(w1_lo_done, k - 1)
                for o in range(KC):
                    last = nc.tensor.transpose(scores[1][:, k % 2, o * P:o * P + P], w1_deq[:, o, k * P:k * P + P], ident[:])
                last.then_inc(w1_ready, 1)

            def effective_b():
                pe.wait_ge(ae_lo_done, 5)
                pe.wait_ge(sh_done, 1)
                for o in range(C):
                    q, m = o % 4, o // 4
                    last = mm(gen[R * q:R * q + R, m // 8, (m % 8) * C:(m % 8) * C + C], lora_b[:, o, :],
                              whole(mix_b[:]), start=True, stop=True)
                last.then_inc(be_ready, 1)

            def make_qk(t):
                pe.wait_ge(cb_lo_done, t + 1)
                pe.wait_ge(ca_done, t + 1)
                if isinstance(t, int) and t == 0:
                    pe.wait_ge(m_done, 3)
                else:
                    pe.wait_ge(numer_done, t)
                    pe.wait_ge(denom_done, t)
                for b in range(2):
                    to = (bank_a, bank_b)[b][0:Q1, :]
                    mm(to, m_hi[:], cb[:, b, :], start=True, stop=False)
                    mm(to, m_lo[:], ca[0:C, b, :], start=False, stop=True).then_inc(qk_ready, 1)

            def natural(t, b, g):
                pe.wait_ge(qa_done, t * 2 + (b + 1))
                if b == 0 and not (isinstance(t, int) and t == 0):
                    if g == 0:
                        pe.wait_ge(k1_done, t)
                        pe.wait_ge(v1_done, t)
                    else:
                        pe.wait_ge(exp_done, t * 4)
                        if isinstance(t, int) and t == 1:
                            pe.wait_ge(w1_lo_done, KC)
                elif b == 1:
                    pe.wait_ge(max_done, t * 4 + (g + 1))
                for j in range(2):
                    c = 2 * g + j
                    last = mm(scores[g][:, j, :], qa[:, b, c * P:c * P + P], ca[:, b, :], start=True, stop=True)
                last.then_inc(nat_ready, 1)

            def max_rows(t, b):
                pe.wait_ge(max_done, t * 4 + (2 * b + 2))
                if b == 0:
                    pe.wait_ge(qb_lo_done, t * 2 + 2)
                else:
                    pe.wait_ge(row_done, t * 2 + 1)
                for c in range(KC):
                    last = nc.tensor.transpose(bank_b[0:1, c * P:c * P + P], neg_max[:, b, c:c + 1], ident[:])
                last.then_inc(row_ready, 1)

            def transposed(t, b, g):
                pe.wait_ge(row_done, t * 2 + (b + 1))
                pe.wait_ge(qb_lo_done, t * 2 + (b + 1))
                pe.wait_ge(qb_hi_done, t * 2 + (b + 1))
                if b == 0:
                    pe.wait_ge(max_done, t * 4 + (g + 3))
                else:
                    pe.wait_ge(exp_done, t * 4 + (g + 1))
                for j in range(2):
                    c = 2 * g + j
                    mm(scores[g][:, j, :], ca[:, b, c * P:c * P + P], qa[:, b, :], start=True, stop=False)
                    last = mm(scores[g][:, j, :], cb[:, b, c * P:c * P + P], qb[:, b, :], start=False, stop=True)
                last.then_inc(tr_ready, 1)

            def make_v0(t):
                pe.wait_ge(ln_done[0], t + 1)
                pe.wait_ge(qb_lo_done, t * 2 + 1)
                for c in range(KC):
                    last = mm(bank_a[:, c * P:c * P + P], norm[0][:, c * P:c * P + P], diag_t[:, V0, :],
                              start=True, stop=True)
                last.then_inc(v0_ready, 1)

            def numerator(t, chunks):
                pe.wait_ge(v0_done, t + 1)
                for c in chunks:
                    if c % 2 == 0:
                        pe.wait_ge(exp_done, t * 4 + (3 + c // 2))
                    for b in range(2):
                        last = mm(bank_a[C * b:C * b + C, :], v0[:, c, C * b:C * b + C], prob[:, b, c, :],
                                  start=(c == 0), stop=(c == KC - 1))
                return last

            def denominator(t):
                pe.wait_ge(sum_done, t * 2 + 2)
                pe.wait_ge(row_done, t * 2 + 2)
                for b in range(2):
                    last = mm(bank_b[C * b:C * b + C, :], ones[:], prob_sum[:, b, :], start=True, stop=True)
                last.then_inc(den_ready, 1)

            def make_k1(t, chunks):
                pe.wait_ge(ctx1_in, t * 16 + 16)
                pe.wait_ge(exp_done, t * 4 + 3)
                for c in chunks:
                    last = mm(scores[0][:, 0, c * P:c * P + P], ctx1[:, c * P:c * P + P], diag_t[:, WK, :], start=True, stop=True)
                return last

            def make_v1(t):
                mm(scores[0][:, 1, :], diag_t[:, WV, :], ctx1[:], start=True, stop=True).then_inc(v1_ready, 1)

            def turn_x(t, Cc):
                pe.wait_ge(ln_done[1], t)
                if isinstance(t, int) and t == 1:
                    pe.wait_ge(be_done, 4)
                if Cc:
                    pe.wait_ge(heads_done, t - 1)
                for c in range(KC):
                    last = nc.tensor.transpose(g6[:, c * P:c * P + P], norm[1][:, c * P:c * P + P], ident[:])
                last.then_inc(xt_ready, 1)

            def low_rank(t, bank):
                pe.wait_ge(low_a_done, t * 2)
                pe.wait_ge(xt_lo_done, t)
                for c in range(KC):
                    for n, (w, x) in enumerate(((low_a_hi, xt_hi), (low_a_lo, xt_hi), (low_a_hi, xt_lo))):
                        last = mm(bank[0:Q1 + 1, 0:P], w[:, c, :], x[:, c, :], start=(c == 0 and n == 0),
                                  stop=(c == KC - 1 and n == 2))
                last.then_inc(low_ready, 1)

            def ffn0_hi(t, bank, chunks):
                pe.wait_ge(xt_hi_done, t)
                if isinstance(t, int) and t == 1:
                    pe.wait_ge(kern_lo_done, 1)
                for c in chunks:
                    mm(bank, xt_hi[:, c, :], kern_hi[:, c, :], start=(c == 0), stop=False)
                    mm(bank, xt_hi[:, c, :], kern_lo[:, c, :], start=False, stop=False)

            def ffn0_lo(t, bank):
                for c in range(KC):
                    mm(bank, xt_lo[:, c, :], kern_hi[:, c, :], start=False, stop=False)
                if isinstance(t, int) and t == 1:
                    pe.wait_ge(low_b_done, 2)
                pe.wait_ge(low_done, t)
                mm(bank, low[:], low_b[:].rearrange("r b o -> r (b o)")[:, bass.ds((t - 1) * T, T)],
                   start=False, stop=True).then_inc(f0_ready, 1)

            def make_q1(t):
                pe.wait_ge(ln_done[2], t)
                for c in range(KC):
                    last = mm(g6[:, c * P:c * P + P], norm[2][:, c * P:c * P + P], diag_t[:, WQ, :], start=True, stop=True)
                last.then_inc(q1_ready, 1)

            def head_scores(t, Cc):
                pe.wait_ge(q1_done, t)
                if Cc:
                    pe.wait_ge(yt_lo_done, t - 1)
                passed(pe)
                for h in range(H):
                    rows = slice(E * (h % 2), E * (h % 2) + E)
                    for b in range(2):
                        cols = slice(C * b, C * b + C)
                        last = mm(gen[cols, h % 2, (h // 2) * E:(h // 2) * E + E], q1t[rows, h // 2, cols],
                                  k1t[rows, h // 2, cols], start=True, stop=True)
                last.then_inc(s1_ready, 1)

            def turn_probs(t):
                pe.wait_ge(pn_done, t)
                passed(pe)
                for n in range(H):
                    last = nc.tensor.transpose(gen[0:E, n // 4, (n % 4) * P:(n % 4) * P + P], prob1[:, n, :], ident[:])
                last.then_inc(pt_ready, 1)

            def head_values(t):
                pe.wait_ge(pt_done, t * 2)
                passed(pe)
                for h in range(H):
                    n = (h % 2) * (H // 2) + h // 2
                    for b in range(2):
                        rows = slice(C * b, C * b + C)
                        last = mm(g6[rows, h * E:h * E + E], prob1t[rows, n, :], v1[rows, h * E:h * E + E],
                                  start=True, stop=True)
                last.then_inc(o1_ready, 1)

            def project(t, bank):
                pe.wait_ge(heads_done, t - 1)
                mm(bank, diag_t[:, WO, :], heads[:], start=True, stop=True).then_inc(wo_ready, 1)

            def turn_y(t, A, B):
                pe.wait_ge(ln_done[3], t - 1)
                if B and not A:
                    pe.wait_ge(low_done, t)
                for c in range(KC):
                    last = nc.tensor.transpose(g7[:, c * P:c * P + P], norm[3][:, c * P:c * P + P], ident[:])
                last.then_inc(yt_ready, 1)

            def ffn1(p, bank, chunks):
                pe.wait_ge(yt_lo_done, p + 1)
                for c in chunks:
                    for n, (x, w) in enumerate(((yt_hi, w1_hi), (yt_hi, w1_lo), (yt_lo, w1_hi))):
                        last = mm(bank, x[:, c, :], w[:, c, :], start=(c == 0 and n == 0), stop=(c == KC - 1 and n == 2))
                return last

            def ffn1_last(p, bank):
                pe.wait_ge(yt_hi_done, p + 1)
                for c in range(KC):
                    mm(bank, yt_hi[:, c, :], w1_hi[:, c, :], start=(c == 0), stop=False)
                    mm(bank, yt_hi[:, c, :], w1_lo[:, c, :], start=False, stop=False)
                pe.wait_ge(yt_lo_done, p + 1)
                for c in range(KC):
                    last = mm(bank, yt_lo[:, c, :], w1_hi[:, c, :], start=False, stop=(c == KC - 1))
                last.then_inc(f1_ready, 1)

            def step(t, A, B, Cc, D, last=False):
                first = isinstance(t, int) and t == 0
                if A:
                    make_qk(t)
                if D:
                    ffn1(t - 3, g7, [0, 1, 2])
                if B and not A:
                    pe.wait_ge(exp_done, 4 * PAIRS)
                    ffn1(PAIRS - 3, tail_ffn1(PAIRS - 3), [0, 1, 2])
                if B:
                    turn_x(t, Cc)
                if D:
                    ffn1(t - 3, g7, [3]).then_inc(f1_ready, 1)
                if Cc and not A:
                    project(t, scores[1][:, 1, :])
                if A:
                    natural(t, 0, 0)
                    natural(t, 0, 1)
                if first:
                    gate_and_wv0()
                if B and not A:
                    pe.wait_ge(numer_done, PAIRS)
                    ffn0_hi(t, ffn0_bank(A), range(KC))
                if A and B:
                    if D:
                        pe.wait_ge(gated_done, t - 2)
                    ffn0_hi(t, ffn0_bank(A), [0, 1, 2])
                if A:
                    natural(t, 1, 0)
                if A and B:
                    ffn0_hi(t, ffn0_bank(A), [3])
                if B:
                    low_rank(t, low_rank_bank(A))
                if A:
                    max_rows(t, 0)
                    natural(t, 1, 1)
                if Cc and A:
                    pe.wait_ge(low_done, t)
                    project(t, g6)
                if first:
                    effective_a(0)
                    turn_diag()
                if B:
                    ffn0_lo(t, ffn0_bank(A))
                if B and not A:
                    ffn1(PAIRS - 3, tail_ffn1(PAIRS - 3), [3]).then_inc(f1_ready, 1)
                if A:
                    transposed(t, 0, 0)
                    max_rows(t, 1)
                    make_v0(t)
                if first:
                    effective_a(1)
                if A:
                    transposed(t, 0, 1)
                if Cc:
                    turn_y(t, A, B)
                if A:
                    transposed(t, 1, 0)
                if B and not A:
                    pe.wait_ge(v1_done, PAIRS)
                    ffn1(PAIRS - 2, tail_ffn1(PAIRS - 2), [0])
                if B:
                    make_q1(t)
                if A:
                    transposed(t, 1, 1)
                if first:
                    effective_a(2)
                if B:
                    head_scores(t, Cc)
                if B and not A:
                    ffn1(PAIRS - 2, tail_ffn1(PAIRS - 2), [1, 2, 3]).then_inc(f1_ready, 1)
                if A:
                    numerator(t, [0, 1])
                    make_k1(t, [0, 1])
                if first:
                    turn_w1(0)
                    turn_w1(1)
                    effective_a(3)
                if A:
                    denominator(t)
                if first:
                    shared()
                if A:
                    make_k1(t, [2, 3]).then_inc(k1_ready, 1)
                    numerator(t, [2])
                if B:
                    turn_probs(t)
                if A:
                    numerator(t, [3]).then_inc(num_ready, 1)
                if first:
                    turn_w1(2)
                    turn_w1(3)
                    effective_b()
                if A:
                    make_v1(t)
                if B:
                    head_values(t)
                if Cc and not B:
                    ffn1_last(PAIRS - 1, tail_ffn1(PAIRS - 1))

            run(pe, before, step)

        @block.vector
        def _(dve):
            v = nc.vector

            def ln_stats(i, src, count):
                v.bn_stats(stats[i][:], src[:]).then_inc(bn_done[i], 1)
                ln_mean_var(i, count)

            def ln_mean_var(i, count):
                dve.wait_ge(bn_done[i], count)
                passed(dve)
                v.bn_aggr(mean_var[i][:], stats[i][:]).then_inc(mv_done[i], 1)

            def ln_apply(i, src, count):
                dve.wait_ge(rstd_done[i], count)
                v.tensor_scalar(norm[i][:], src[:], mean_var[i][:, 0:1], rstd[i][:], ALU.subtract,
                                ALU.mult).then_inc(ln_done[i], 1)

            def add_last_pair(t):
                dve.wait_ge(exp_done, t * 4 + 4)
                dve.wait_ge(sum_done, t * 2 + 1)
                v.tensor_tensor(half[:, 1, :], prob[:, 1, 2, :], prob[:, 1, 3, :], ALU.add).then_inc(last_half_done, 1)

            def add_pairs(t, b):
                if b == 0:
                    dve.wait_ge(half_done, t * 3 + 2)
                else:
                    dve.wait_ge(half_done, t * 3 + 3)
                    dve.wait_ge(last_half_done, t + 1)
                v.tensor_tensor(prob_sum[:, b, :], half[:, 0, :], half[:, 1, :], ALU.add).then_inc(sum_done, 1)

            def before():
                v.memset(diag[0:C, :, C:P], 0.0)
                v.memset(diag[C:P, :, 0:C], 0.0)
                v.memset(ca[C:Q1].bitcast(F32), 1.0)
                v.memset(low[C:Q1, :], 1.0).then_inc(dve_const, 1)
                dve.wait_ge(pool_const, 2)
                v.tensor_reduce(eq_r[:], ident[:].rearrange("p (q r) -> p r q", q=4), AX.X, ALU.add).then_inc(gate_done, 1)
                v.tensor_reduce(eq_o[:], ident[:].rearrange("p (n o) -> p o n", n=NL), AX.X, ALU.add).then_inc(gate_done, 1)
                dve.wait_ge(m_ready, 1)
                v.tensor_copy(m_hi[:], bank_a[:, 0:Q1]).then_inc(m_hi_done, 1)
                dve.wait_ge(m_ready, 2)
                v.tensor_copy(qk_bias[:], bank_b[0:Q1, 0:1]).then_inc(m_done, 1)
                dve.wait_ge(m_hi_done, 1)
                v.tensor_tensor(m_lo[:], bank_a[0:C, 0:Q1], m_hi[0:C, :].bitcast(F32), ALU.subtract).then_inc(m_done, 2)
                dve.wait_ge(cb_hi_done, 1)
                v.tensor_tensor(cb[0:C], ctx2[0:C], cb[0:C].bitcast(F32), ALU.subtract).then_inc(cb_lo_done, 1)
                dve.wait_ge(x_ln_in, 16)
                ln_stats(0, x_ln, 1)
                ln_apply(0, x_ln, 1)

            def gate_and_wv0():
                dve.wait_ge(tg_done, 1)
                dve.wait_ge(gate_ready, 1)
                v.tensor_scalar(diag_t[:, V0, :], g6[:, P:2 * P], tg[:, GX0:GX0 + 1], None, ALU.mult).then_inc(diag_done, 1)
                v.tensor_scalar(bv0_col[:], bv0_col[:], tg[:, GX0:GX0 + 1], None, ALU.mult).then_inc(row_bias_done, 1)
                v.tensor_copy(gate_p[:], g6[:, 0:5 * PAIRS]).then_inc(gate_done, 1)
                dve.wait_ge(gate_done, 3)
                v.tensor_tensor(mix_a[:], gate_p[:, 0:KC * PAIRS].unsqueeze(2).broadcast_to([P, KC * PAIRS, R]),
                                eq_r[:].unsqueeze(1).broadcast_to([P, KC * PAIRS, R]), ALU.mult).then_inc(mix_done, 1)
                v.tensor_tensor(mix_b[:], gate_p[:, KC * PAIRS:].unsqueeze(2).broadcast_to([P, PAIRS, PAIRS]),
                                eq_o[:].unsqueeze(1).broadcast_to([P, PAIRS, PAIRS]), ALU.mult).then_inc(mix_done, 1)

            def turned_diag():
                dve.wait_ge(diag_ready, 1)
                for n in (WQ, WK, WV):
                    v.tensor_copy(diag_t[:, n, :], g7[:, (n - 1) * P:n * P]).then_inc(diag_done, 1)
                v.tensor_scalar(diag_t[:, WO, :], g7[:, (WO - 1) * P:WO * P], tg[:, GX1:GX1 + 1], None,
                                ALU.mult).then_inc(diag_done, 1)
                v.tensor_scalar(bo_col[:], bo_col[:], tg[:, GX1:GX1 + 1], None, ALU.mult).then_inc(row_bias_done, 1)

            def effective_a(k):
                dve.wait_ge(ae_hi_done, k + 1)
                v.tensor_tensor(ae_lo[:, :, k, :], gen[:, k % 2, 0:PAIRS * R].rearrange("p (b r) -> p b r", b=PAIRS),
                                ae_hi[:, :, k, :].bitcast(F32), ALU.subtract).then_inc(ae_lo_done, 1)

            def shared():
                dve.wait_ge(ae_hi_done, KC + 1)
                v.tensor_tensor(low_a_lo[:, :, R:2 * R], g6[:, 0:P].rearrange("p (k r) -> p k r", k=KC),
                                low_a_hi[:, :, R:2 * R].bitcast(F32), ALU.subtract).then_inc(ae_lo_done, 1)
                dve.wait_ge(sh_ready, 2)
                v.tensor_copy(share_bt[R:2 * R, :], g7[0:R, :]).then_inc(sh_done, 1)

            def spread_shared_b():
                dve.wait_ge(sh_done, 1)
                v.tensor_copy(low_b[R:2 * R, 0:PAIRS // 2],
                              share_bt[R:2 * R, :].unsqueeze(1).broadcast_to([R, PAIRS // 2, T])).then_inc(low_b_done, 1)

            def dequantise_w1():
                dve.wait_ge(w_ffn1, 16 * N_FFN1)
                for k in range(KC):
                    v.tensor_tensor(w1_deq[:, k, :].rearrange("p (j i) -> p j i", i=QB_),
                                    q8[:, k, :].rearrange("p (j i) -> p j i", i=QB_),
                                    q_scale[:, k, :].unsqueeze(2).broadcast_to([P, T // QB_, QB_]), ALU.mult).then_inc(w1_deq_done, 1)
                v.tensor_scalar(b1_row[:], b1_row[:], tg[:, GF1:GF1 + 1], None, ALU.mult).then_inc(b1_done, 1)

            def turned_w1(k):
                dve.wait_ge(w1_hi_done, k + 1)
                v.tensor_tensor(w1_lo[:, k, :], scores[1][:, k % 2, :], w1_hi[:, k, :].bitcast(F32),
                                ALU.subtract).then_inc(w1_lo_done, 1)

            def effective_b(q):
                dve.wait_ge(be_ready, 1)
                v.tensor_copy(low_b[0:R].rearrange("r b (a m q) -> r (b a) m q", a=PAIRS, q=4)[:, :, :, q],
                              gen[R * q:R * q + R].rearrange("r g (m x) -> r x (g m)", x=C)).then_inc(be_done, 1)

            def output_projected(t, bank, again):
                dve.wait_ge(wo_ready, t - 1)
                if again:
                    dve.wait_ge(x3b_done, t - 2)
                v.scalar_tensor_tensor(out=x3[:], in0=bank, scalar=bo_col[:], in1=x2[:], op0=ALU.add,
                                       op1=ALU.add).then_inc(x3_done, 1)

            def turned_y(t):
                dve.wait_ge(yt_hi_done, t - 1)
                v.tensor_tensor(whole(yt_lo[:]), g7, whole(yt_hi[:]).bitcast(F32), ALU.subtract).then_inc(yt_lo_done, 1)

            def finish(p):
                dve.wait_ge(x3b_done, p + 1)
                dve.wait_ge(stored, 16 * (p + 1))
                dve.wait_ge(f1_ready, p + 1)
                v.scalar_tensor_tensor(out=x4[:], in0=tail_ffn1(p), scalar=tg[:, GF1:GF1 + 1], in1=x3b[:],
                                       op0=ALU.mult, op1=ALU.add).then_inc(x4_done, 1)

            def maximum(t, b, g):
                dve.wait_ge(nat_ready, t * 4 + (2 * b + g + 1))
                v.tensor_reduce(neg_max[:, b, 2 * g:2 * g + 2], scores[g][:], AX.X, ALU.max,
                                negate=True).then_inc(max_done, 1)

            def invert_denominator(t):
                dve.wait_ge(denom_done, t + 1)
                v.reciprocal(recip[:], denom[:]).then_inc(recip_done, 1)

            def shift_row(t, b):
                dve.wait_ge(row_ready, t * 2 + (b + 1))
                v.tensor_tensor(qa[C:Q1, b, :], bank_b[0:1, :], qa[C:Q1, b, :].bitcast(F32), ALU.add).then_inc(row_done, 1)

            def step(t, A, B, Cc, D, last=False):
                first = isinstance(t, int) and t == 0
                if A:
                    for b in range(2):
                        dve.wait_ge(qa_done, t * 2 + (b + 1))
                        v.scalar_tensor_tensor(out=qb[C:P, b, :], in0=(bank_a, bank_b)[b][0:C, :], scalar=qk_bias[0:C, :],
                                               in1=qa[0:C, b, :].bitcast(F32), op0=ALU.add, op1=ALU.subtract).then_inc(qb_lo_done, 1)
                if B:
                    dve.wait_ge(xt_hi_done, t)
                    v.tensor_tensor(whole(xt_lo[:]), g6, whole(xt_hi[:]).bitcast(F32), ALU.subtract).then_inc(xt_lo_done, 1)
                if A:
                    maximum(t, 0, 0)
                    maximum(t, 0, 1)
                if isinstance(t, int) and t == 1:
                    spread_shared_b()
                if first:
                    gate_and_wv0()
                if A:
                    maximum(t, 1, 0)
                    shift_row(t, 0)
                    maximum(t, 1, 1)
                if Cc:
                    output_projected(t, g6 if A else scores[1][:, 1, :], D or not A)
                if first:
                    effective_a(0)
                    turned_diag()
                if Cc:
                    dve.wait_ge(x3_done, t - 1)
                    v.bn_stats(stats[3][:], x3[:]).then_inc(bn_done[3], 1)
                if Cc and not A:
                    ln_mean_var(3, t - 1)
                if B and not A:
                    ln_apply(3, x3, t - 1)
                if B:
                    dve.wait_ge(f0_ready, t)
                    v.scalar_tensor_tensor(out=x2[:], in0=ffn0_bank(A), scalar=tg[:, GF0:GF0 + 1], in1=x1[:], op0=ALU.mult,
                                           op1=ALU.add).then_inc(x2_done, 1)
                    if Cc and A:
                        ln_mean_var(3, t - 1)
                    dve.wait_ge(x2_done, t)
                    v.bn_stats(stats[2][:], x2[:]).then_inc(bn_done[2], 1)
                    if A:
                        shift_row(t, 1)
                    ln_mean_var(2, t)
                if A and not B:
                    shift_row(t, 1)
                if Cc and (A or not B):
                    ln_apply(3, x3, t - 1)
                if Cc and not B:
                    finish(PAIRS - 2)
                if first:
                    dequantise_w1()
                    effective_a(1)
                if B and not A:
                    turned_y(t)
                if B:
                    ln_apply(2, x2, t)
                if A and not last:
                    dve.wait_ge(x_ln_in, t * 16 + 32)
                    ln_stats(0, x_ln, t + 2)
                if Cc and (A or not B):
                    turned_y(t)
                if B:
                    dve.wait_ge(q1_ready, t)
                    v.tensor_tensor(q1t[:], g6.rearrange("p (k m) -> p k m", k=KC),
                                    whole(bq1_row[:]).unsqueeze(1).broadcast_to([P, KC, P]), ALU.add).then_inc(q1_done, 1)
                if B and not A:
                    finish(PAIRS - 3)
                if A:
                    add_pairs(t, 0)
                if A and not last:
                    dve.wait_ge(v0_ready, t + 1)
                    ln_apply(0, x_ln, t + 2)
                if A:
                    add_last_pair(t)
                if B:
                    dve.wait_ge(s1_ready, t)
                    s1 = gen[:, :, 0:H // 2 * E].rearrange("p g (h e) -> p g h e", e=E)
                    v.tensor_reduce(head_max[:].rearrange("p (g h) -> p g h", g=2), s1, AX.X, ALU.max).then_inc(hmax_done, 1)
                    dve.wait_ge(hmax_done, t)
                    v.tensor_tensor(shifted[:].rearrange("p (g h) e -> p g h e", g=2), s1,
                                    head_max[:].rearrange("p (g h) -> p g h", g=2).unsqueeze(3).broadcast_to([P, 2, H // 2, E]),
                                    ALU.subtract).then_inc(shift_done, 1)
                if A:
                    add_pairs(t, 1)
                if first:
                    effective_a(2)
                    turned_w1(0)
                    turned_w1(1)
                    effective_a(3)
                    shared()
                    invert_denominator(t)
                    turned_w1(2)
                    turned_w1(3)
                if B:
                    dve.wait_ge(p1_done, t)
                    v.tensor_reduce(head_sum[:], prob1[:], AX.X, ALU.add).then_inc(hsum_done, 1)
                    dve.wait_ge(hsum_done, t)
                    v.reciprocal(head_rec[:], head_sum[:]).then_inc(hrec_done, 1)
                    dve.wait_ge(hrec_done, t)
                    v.tensor_tensor(prob1[:], prob1[:], head_rec[:].unsqueeze(2).broadcast_to([P, H, E]),
                                    ALU.mult).then_inc(pn_done, 1)
                if Cc and not B:
                    finish(PAIRS - 1)
                if A:
                    if not first:
                        invert_denominator(t)
                    dve.wait_ge(recip_done, t + 1)
                    dve.wait_ge(numer_done, t + 1)
                    v.tensor_tensor(att[:], numer[:], recip[:], ALU.mult).then_inc(att_done, 1)
                    dve.wait_ge(att_done, t + 1)
                    dve.wait_ge(x_res_in, t * 16 + 16)
                    if isinstance(t, int) and t == 0:
                        dve.wait_ge(row_bias_done, 1)
                    v.scalar_tensor_tensor(out=x1[:], in0=att[:], scalar=bv0_col[:], in1=x_res[:],
                                           op0=ALU.add, op1=ALU.add).then_inc(x1_done, 1)
                    dve.wait_ge(x1_done, t + 1)
                    ln_stats(1, x1, t + 1)
                    if first:
                        effective_b(0)
                        ln_apply(1, x1, t + 1)
                    dve.wait_ge(k1_ready, t + 1)
                    v.tensor_tensor(k1t[:], scores[0][:, 0, :].rearrange("p (k m) -> p k m", k=KC),
                                    whole(bk1_row[:]).unsqueeze(1).broadcast_to([P, KC, P]), ALU.add).then_inc(k1_done, 1)
                    if not first:
                        ln_apply(1, x1, t + 1)

            run(dve, before, step)

        @block.gpsimd
        def _(pool):
            g = nc.gpsimd

            def ln_rstd(i, count):
                pool.wait_ge(mv_done[i], count)
                passed(pool)
                g.tensor_scalar(var_eps[i][:], mean_var[i][:, 1:2], EPS, 1.0, ALU.add, ALU.mult).then_inc(eps_done[i], 1)
                pool.wait_ge(eps_done[i], count)
                g.tensor_tensor(rstd[i][:], var_eps[i][:], neg_half[:], ALU.pow).then_inc(rstd_done[i], 1)

            def add_pair(t, b, k):
                if k == 0 and not (b == 0 and isinstance(t, int) and t == 0):
                    pool.wait_ge(sum_done, t * 2 + b)
                pool.wait_ge(exp_done, t * 4 + (2 * b + k + 1))
                g.tensor_tensor(half[:, k, :], prob[:, b, 2 * k, :], prob[:, b, 2 * k + 1, :], ALU.add).then_inc(half_done, 1)

            def split_ctx_low(p):
                pool.wait_ge(cb_hi_done, p + 1)
                g.tensor_tensor(cb[0:C], ctx2[0:C], cb[0:C].bitcast(F32), ALU.subtract).then_inc(cb_lo_done, 1)

            def before():
                g.memset(neg_half[:], -0.5)
                g.memset(ones[:], 1.0)
                g.memset(low_a_hi[:, :, 2 * R:].bitcast(F32), 0.0)
                g.memset(low_a_lo[:, :, 2 * R:].bitcast(F32), 0.0)
                g.memset(sel_a[:], 0.0).then_inc(pool_zero, 1)
                g.memset(sel_b[:], 0.0).then_inc(pool_zero, 1)
                g.memset(ident[:], 0.0).then_inc(pool_zero, 1)
                pool.wait_ge(pool_zero, 3)
                g.affine_select(out=ident[:], in_=ident[:], compare_op=ALU.not_equal, fill=1.0, base=0,
                                pattern=[[-1, P]], channel_multiplier=1).then_inc(pool_const, 1)
                g.affine_select(out=sel_a[:], in_=sel_a[:], compare_op=ALU.not_equal, fill=1.0, base=0,
                                pattern=[[-4, KC], [-1, 4], [0, R]], channel_multiplier=1)
                g.affine_select(out=sel_b[:], in_=sel_b[:], compare_op=ALU.not_equal, fill=1.0, base=0,
                                pattern=[[-1, NL], [0, PAIRS]], channel_multiplier=1).then_inc(pool_const, 1)
                ln_rstd(0, 1)

            def step(t, A, B, Cc, D, last=False):
                first = isinstance(t, int) and t == 0
                if B:
                    if isinstance(t, int) and t == 1:
                        pool.wait_ge(ae_lo_done, 5)
                        pool.wait_ge(ae_hi_done, 5)
                    else:
                        pool.wait_ge(low_ready, t - 1)
                    for full, part in ((ae_hi, low_a_hi), (ae_lo, low_a_lo)):
                        g.tensor_copy(part[:, :, 0:R],
                                      full[:].rearrange("p b k r -> p (b k r)")[:, bass.ds((t - 1) * KC * R, KC * R)]
                                      .rearrange("p (k r) -> p k r", k=KC).bitcast(F32)).then_inc(low_a_done, 1)
                if D:
                    pool.wait_ge(x3b_done, t - 2)
                    pool.wait_ge(gated_done, t - 2)
                    pool.wait_ge(stored, t * 16 - 32)
                    g.tensor_tensor(x4[:], ffn1_gated[:], x3b[:], ALU.add).then_inc(x4_done, 1)
                if Cc:
                    ln_rstd(3, t - 1)
                if B:
                    ln_rstd(2, t)
                if A:
                    add_pair(t, 0, 0)
                    add_pair(t, 0, 1)
                if A and not last:
                    ln_rstd(0, t + 2)
                if A:
                    add_pair(t, 1, 0)
                if first:
                    pool.wait_ge(kern_hi_done, 1)
                    g.tensor_tensor(kern_lo[:], kern[:], kern_hi[:].bitcast(F32), ALU.subtract).then_inc(kern_lo_done, 1)
                if A and not last:
                    split_ctx_low(t + 1)
                if Cc:
                    if isinstance(t, int) and t == 2:
                        pool.wait_ge(b1_done, 1)
                    if not A:
                        pool.wait_ge(x4_done, t - 2)
                    g.tensor_tensor(x3b[:], x3[:], b1_row[:], ALU.add).then_inc(x3b_done, 1)
                if A:
                    ln_rstd(1, t + 1)

            run(pool, before, step)


_INS = ["x", "ctx_4096", "g_xattn", "g_ffn", "L0_xattn_Wq", "L0_xattn_bq", "L0_xattn_Wk", "L0_xattn_bk",
        "L0_xattn_Wv", "L0_xattn_bv", "L0_ffn_gate", "L0_ffn_kernel", "L0_ffn_bias", "L0_ffn_lora_A",
        "L0_ffn_lora_B", "L0_ffn_lora_A_shared", "L0_ffn_lora_B_shared", "L1_xattn_Wq", "L1_xattn_bq",
        "L1_xattn_Wk", "L1_xattn_bk", "L1_xattn_Wv", "L1_xattn_bv", "L1_xattn_Wo", "L1_xattn_bo",
        "L1_ffn_quantized_weights", "L1_ffn_scale_values", "L1_ffn_bias"]


def kernel(**inputs):
    import numpy as _np
    import concourse.bacc as _bacc
    from concourse import mybir as _mybir
    from concourse.bass_utils import run_bass_kernel_spmd as _run

    nc = _bacc.Bacc("TRN2", target_bir_lowering=False, num_devices=1)
    arrays, args = {}, {}
    for name in _INS:
        arr = _np.ascontiguousarray(inputs[name])
        if arr.dtype == _np.int8:
            arr = arr.view(_np.int32)
        arrays[f"in_{name}"] = arr
        args[name] = nc.dram_tensor(f"in_{name}", arr.shape, _mybir.dt.from_np(arr.dtype), kind="ExternalInput").ap()
    out = nc.dram_tensor("out_x", (NB, C, T), _mybir.dt.float32, kind="ExternalOutput").ap()
    flamingo_two_layers(nc, args, out)
    r = _run(nc, [arrays], core_ids=[0])
    return r.results[0]["out_x"]
```
